# Optimizing a Trainium2 kernel written in Bass

```python
import numpy as np
import jax
import jax.numpy as jnp

def _softmax(x, axis=-1):
    return jax.nn.softmax(x, axis=axis)

def _gelu(x):
    return jax.nn.gelu(x, approximate=True)

def _silu(x):
    return jax.nn.silu(x)

def _sigmoid(x):
    return jax.nn.sigmoid(x)

def _layernorm(x, axis=-1, eps=1e-05):
    m = jnp.mean(x, axis=axis, keepdims=True)
    v = jnp.var(x, axis=axis, keepdims=True)
    return (x - m) / jnp.sqrt(v + eps)

def _scatter_add(tgt, idx, src, axis=0):
    return tgt.at[idx].add(src)

def _segment_sum(src, seg, n):
    return jax.ops.segment_sum(src, seg, n)
kernel_name = 'mk_audio_tower_d2_tok_audfeat768_r4_39db81'

def setup_inputs(seed: int=0):
    np.random.seed(seed)
    _w = jnp.asarray

    def _rec_inputs():
        import jax
        import jax.numpy as jnp
        _rk = jax.random.key(seed)
        x = -0.000222058 + 0.999998 * jax.random.normal(jax.random.fold_in(_rk, 1), (64, 125, 192), jnp.float32)
        return x
    x = _rec_inputs()

    def _L0_tok_setup():
        import jax, jax.numpy as jnp
        import numpy as np
        B, S, D, K = (8, 1024, 192, 7)
        EPS = 1e-05
        key = jax.random.key(seed)
        k0, k1, k2, k3, k4 = jax.random.split(key, 5)
        return {'x': jax.random.normal(k0, (B, S, D), jnp.float32), 'w_dw': jax.random.normal(k1, (D, 1, K), jnp.float32) * 0.2, 'b_dw': jax.random.normal(k2, (D,), jnp.float32) * 0.02, 'w_pw': jax.random.normal(k3, (D, D, 1), jnp.float32) * 0.03, 'b_pw': jax.random.normal(k4, (D,), jnp.float32) * 0.02, 'gamma': jnp.ones((D,), jnp.float32), 'beta': jnp.zeros((D,), jnp.float32)}
    _L0_tok_all = _L0_tok_setup()
    _L0_tok_in = {k: v for k, v in _L0_tok_all.items() if k in ('w_dw', 'b_dw', 'w_pw', 'b_pw', 'gamma', 'beta')}
    del _L0_tok_all

    def _L0_attn_setup():
        import jax, jax.numpy as jnp
        import numpy as np
        B, T, D = (2, 512, 192)
        H, K, V = (8, 64, 96)
        F = 32

        def positional_features(positions, feature_size, seq_length):
            nb = feature_size // 2
            pow_rate = np.exp(np.log(seq_length + 1) / nb).astype(np.float32)
            center_widths = pow_rate ** jnp.arange(1, nb + 1, dtype=jnp.float32) - 1.0
            emb = (center_widths[None, :] > jnp.abs(positions)[:, None]).astype(jnp.float32)
            return jnp.concatenate([emb, jnp.sign(positions)[:, None] * emb], axis=-1)

        def relative_shift(x):
            b, h, t1, t2 = x.shape
            x = jnp.pad(x, ((0, 0), (0, 0), (0, 0), (1, 0)))
            x = x.reshape(b, h, t2 + 1, t1)[:, :, 1:, :].reshape(b, h, t1, t2)
            return x[..., :(t2 + 1) // 2]
        key = jax.random.key(seed)
        ks = jax.random.split(key, 9)
        w = lambda k, shape: jax.random.normal(k, shape, jnp.float32) * 0.02
        return {'x': jax.random.normal(ks[0], (B, T, D), jnp.float32), 'Wq': w(ks[1], (D, H * K)), 'Wk': w(ks[2], (D, H * K)), 'Wv': w(ks[3], (D, H * V)), 'Wrk': w(ks[4], (F, H * K)), 'r_w_bias': w(ks[5], (H, K)), 'r_r_bias': w(ks[6], (H, K)), 'Wo': w(ks[7], (H * V, D)), 'bo': jnp.zeros((D,), jnp.float32)}
    _L0_attn_all = _L0_attn_setup()
    _L0_attn_in = {k: v for k, v in _L0_attn_all.items() if k in ('Wq', 'Wk', 'Wv', 'Wrk', 'r_w_bias', 'r_r_bias', 'Wo', 'bo')}
    del _L0_attn_all

    def _L0_ffn_setup():
        import jax, jax.numpy as jnp
        import numpy as np
        EPS_NORM = 1e-06
        EPS_Q = 1e-05

        def rmsnorm(x, g):
            return x * jax.lax.rsqrt(jnp.mean(x * x, axis=-1, keepdims=True) + EPS_NORM) * g

        def activation_quant(x):
            scale = 127.0 / jnp.maximum(jnp.max(jnp.abs(x), axis=-1, keepdims=True), EPS_Q)
            return jnp.clip(jnp.round(x * scale), -128, 127) / scale

        def weight_quant(w):
            scale = 1.0 / jnp.maximum(jnp.mean(jnp.abs(w)), EPS_Q)
            return jnp.clip(jnp.round(w * scale), -1, 1) / scale

        def bitlinear(x, w, g):
            x_norm = rmsnorm(x, g)
            x_q = x_norm + jax.lax.stop_gradient(activation_quant(x_norm) - x_norm)
            w_q = w + jax.lax.stop_gradient(weight_quant(w) - w)
            return jnp.einsum('bsd,od->bso', x_q, w_q)
        key = jax.random.key(seed)
        k1, k2, k3 = jax.random.split(key, 3)
        B, S, D, H = (8, 1024, 192, 512)
        x = jax.random.normal(k1, (B, S, D), dtype=jnp.float32)
        w_in = jax.random.normal(k2, (2 * H, D), dtype=jnp.float32) * 0.002
        w_out = jax.random.normal(k3, (D, H), dtype=jnp.float32) * 0.002
        g_in = jnp.ones((D,), dtype=jnp.float32)
        g_out = jnp.ones((H,), dtype=jnp.float32)
        return {'x': x, 'w_in': w_in, 'g_in': g_in, 'w_out': w_out, 'g_out': g_out}
    _L0_ffn_all = _L0_ffn_setup()
    _L0_ffn_in = {k: v for k, v in _L0_ffn_all.items() if k in ('w_in', 'g_in', 'w_out', 'g_out')}
    del _L0_ffn_all

    def _L1_attn_setup():
        import jax, jax.numpy as jnp
        import numpy as np
        N_EMBD = 192
        N_HEAD = 12
        N_KV_HEAD = 4
        NUM_KV_HEADS = N_HEAD // N_KV_HEAD
        HEAD_DIM = N_EMBD // N_HEAD
        BLOCK_SIZE = 256
        SCALE = (HEAD_DIM * N_KV_HEAD / N_HEAD) ** (-0.5)

        def _rotary_cos_sin(T, d, dtype):
            inv_freq = 1.0 / 10000.0 ** (jnp.arange(0, d, 2, dtype=jnp.float32) / d)
            t = jnp.arange(T, dtype=jnp.float32)
            freqs = jnp.outer(t, inv_freq)
            return (jnp.cos(freqs).astype(dtype)[None, None], jnp.sin(freqs).astype(dtype)[None, None])

        def _apply_rotary(x):
            T, d = (x.shape[2], x.shape[3])
            cos, sin = _rotary_cos_sin(T, d, x.dtype)
            x1, x2 = (x[..., :d // 2], x[..., d // 2:])
            return jnp.concatenate([x1 * cos - x2 * sin, x1 * sin + x2 * cos], axis=-1)
        key = jax.random.key(seed)
        k0, k1, k2, k3, k4 = jax.random.split(key, 5)
        b, T = (2, 512)
        s = 0.02
        return {'hidden_states': jax.random.normal(k0, (b, T, N_EMBD), jnp.float32), 'Wq': jax.random.normal(k1, (N_HEAD * HEAD_DIM, N_EMBD), jnp.float32) * s, 'Wk': jax.random.normal(k2, (NUM_KV_HEADS * HEAD_DIM, N_EMBD), jnp.float32) * s, 'Wv': jax.random.normal(k3, (NUM_KV_HEADS * HEAD_DIM, N_EMBD), jnp.float32) * s, 'Wo': jax.random.normal(k4, (N_EMBD, N_HEAD * HEAD_DIM), jnp.float32) * s}
    _L1_attn_all = _L1_attn_setup()
    _L1_attn_in = {k: v for k, v in _L1_attn_all.items() if k in ('Wq', 'Wk', 'Wv', 'Wo')}
    del _L1_attn_all

    def _L1_ffn_setup():
        import jax, jax.numpy as jnp
        import numpy as np
        S, B, DIM = (256, 4, 192)
        N_EXPERTS = 8
        HID = 512
        key = jax.random.key(seed)
        ks = jax.random.split(key, 6)
        scale = 0.02
        return {'hidden_states': jax.random.normal(ks[0], (S, B, DIM), dtype=jnp.float32), 'router_w': jax.random.normal(ks[1], (DIM, N_EXPERTS), dtype=jnp.float32) * scale, 'router_b': jnp.zeros((N_EXPERTS,), dtype=jnp.float32), 'w1': jax.random.normal(ks[2], (N_EXPERTS, DIM, HID), dtype=jnp.float32) * scale, 'w2': jax.random.normal(ks[3], (N_EXPERTS, DIM, HID), dtype=jnp.float32) * scale, 'w3': jax.random.normal(ks[4], (N_EXPERTS, HID, DIM), dtype=jnp.float32) * scale}
    _L1_ffn_all = _L1_ffn_setup()
    _L1_ffn_in = {k: v for k, v in _L1_ffn_all.items() if k in ('router_w', 'router_b', 'w1', 'w2', 'w3')}
    del _L1_ffn_all
    return {'x': x, 'L0_tok_w_dw': _L0_tok_in['w_dw'], 'L0_tok_b_dw': _L0_tok_in['b_dw'], 'L0_tok_w_pw': _L0_tok_in['w_pw'], 'L0_tok_b_pw': _L0_tok_in['b_pw'], 'L0_tok_gamma': _L0_tok_in['gamma'], 'L0_tok_beta': _L0_tok_in['beta'], 'L0_attn_Wq': _L0_attn_in['Wq'], 'L0_attn_Wk': _L0_attn_in['Wk'], 'L0_attn_Wv': _L0_attn_in['Wv'], 'L0_attn_Wrk': _L0_attn_in['Wrk'], 'L0_attn_r_w_bias': _L0_attn_in['r_w_bias'], 'L0_attn_r_r_bias': _L0_attn_in['r_r_bias'], 'L0_attn_Wo': _L0_attn_in['Wo'], 'L0_attn_bo': _L0_attn_in['bo'], 'L0_ffn_w_in': _L0_ffn_in['w_in'], 'L0_ffn_g_in': _L0_ffn_in['g_in'], 'L0_ffn_w_out': _L0_ffn_in['w_out'], 'L0_ffn_g_out': _L0_ffn_in['g_out'], 'L1_attn_Wq': _L1_attn_in['Wq'], 'L1_attn_Wk': _L1_attn_in['Wk'], 'L1_attn_Wv': _L1_attn_in['Wv'], 'L1_attn_Wo': _L1_attn_in['Wo'], 'L1_ffn_router_w': _L1_ffn_in['router_w'], 'L1_ffn_router_b': _L1_ffn_in['router_b'], 'L1_ffn_w1': _L1_ffn_in['w1'], 'L1_ffn_w2': _L1_ffn_in['w2'], 'L1_ffn_w3': _L1_ffn_in['w3']}

def reference(x, L0_tok_w_dw, L0_tok_b_dw, L0_tok_w_pw, L0_tok_b_pw, L0_tok_gamma, L0_tok_beta, L0_attn_Wq, L0_attn_Wk, L0_attn_Wv, L0_attn_Wrk, L0_attn_r_w_bias, L0_attn_r_r_bias, L0_attn_Wo, L0_attn_bo, L0_ffn_w_in, L0_ffn_g_in, L0_ffn_w_out, L0_ffn_g_out, L1_attn_Wq, L1_attn_Wk, L1_attn_Wv, L1_attn_Wo, L1_ffn_router_w, L1_ffn_router_b, L1_ffn_w1, L1_ffn_w2, L1_ffn_w3):
    import jax
    import jax.numpy as jnp

    def _L0_tok_ref(x, w_dw, b_dw, w_pw, b_pw, gamma, beta):
        import jax, jax.numpy as jnp
        import numpy as np
        B, S, D, K = (8, 1024, 192, 7)
        EPS = 1e-05
        d = w_dw.shape[0]
        h = jnp.transpose(x, (0, 2, 1))
        h = jax.lax.conv_general_dilated(h, w_dw, window_strides=(1,), padding='SAME', dimension_numbers=('NCH', 'OIH', 'NCH'), feature_group_count=d) + b_dw[None, :, None]
        h = jnp.einsum('od,bds->bos', w_pw[:, :, 0], h) + b_pw[None, :, None]
        h = jax.nn.relu(h)
        h = jax.lax.reduce_window(h, -jnp.inf, jax.lax.max, (1, 1, 2), (1, 1, 2), 'VALID')
        h = jnp.transpose(h, (0, 2, 1))
        y = jnp.real(jnp.fft.fft2(h))
        mu = jnp.mean(y, axis=-1, keepdims=True)
        var = jnp.var(y, axis=-1, keepdims=True)
        return (y - mu) * jax.lax.rsqrt(var + EPS) * gamma + beta

    def _L0_attn_ref(x, Wq, Wk, Wv, Wrk, r_w_bias, r_r_bias, Wo, bo):
        import jax, jax.numpy as jnp
        import numpy as np
        B, T, D = (2, 512, 192)
        H, K, V = (8, 64, 96)
        F = 32

        def positional_features(positions, feature_size, seq_length):
            nb = feature_size // 2
            pow_rate = np.exp(np.log(seq_length + 1) / nb).astype(np.float32)
            center_widths = pow_rate ** jnp.arange(1, nb + 1, dtype=jnp.float32) - 1.0
            emb = (center_widths[None, :] > jnp.abs(positions)[:, None]).astype(jnp.float32)
            return jnp.concatenate([emb, jnp.sign(positions)[:, None] * emb], axis=-1)

        def relative_shift(x):
            b, h, t1, t2 = x.shape
            x = jnp.pad(x, ((0, 0), (0, 0), (0, 0), (1, 0)))
            x = x.reshape(b, h, t2 + 1, t1)[:, :, 1:, :].reshape(b, h, t1, t2)
            return x[..., :(t2 + 1) // 2]
        b, t, _ = x.shape
        q = (x @ Wq).reshape(b, t, H, K).transpose(0, 2, 1, 3) * K ** (-0.5)
        k = (x @ Wk).reshape(b, t, H, K).transpose(0, 2, 1, 3)
        v = (x @ Wv).reshape(b, t, H, V).transpose(0, 2, 1, 3)
        content = jnp.einsum('bhtk,bhsk->bhts', q + r_w_bias[None, :, None, :], k)
        positions = jnp.arange(-t + 1, t, dtype=jnp.float32)
        pos_emb = positional_features(positions, F, t)
        r_k = (pos_emb @ Wrk).reshape(2 * t - 1, H, K)
        rel = jnp.einsum('bhtk,rhk->bhtr', q + r_r_bias[None, :, None, :], r_k)
        rel = relative_shift(rel)
        attn = jax.nn.softmax(content + rel, axis=-1)
        out = jnp.einsum('bhts,bhsv->bhtv', attn, v)
        out = out.transpose(0, 2, 1, 3).reshape(b, t, H * V)
        return out @ Wo + bo

    def _L0_ffn_ref(x, w_in, g_in, w_out, g_out):
        import jax, jax.numpy as jnp
        import numpy as np
        EPS_NORM = 1e-06
        EPS_Q = 1e-05

        def rmsnorm(x, g):
            return x * jax.lax.rsqrt(jnp.mean(x * x, axis=-1, keepdims=True) + EPS_NORM) * g

        def activation_quant(x):
            scale = 127.0 / jnp.maximum(jnp.max(jnp.abs(x), axis=-1, keepdims=True), EPS_Q)
            return jnp.clip(jnp.round(x * scale), -128, 127) / scale

        def weight_quant(w):
            scale = 1.0 / jnp.maximum(jnp.mean(jnp.abs(w)), EPS_Q)
            return jnp.clip(jnp.round(w * scale), -1, 1) / scale

        def bitlinear(x, w, g):
            x_norm = rmsnorm(x, g)
            x_q = x_norm + jax.lax.stop_gradient(activation_quant(x_norm) - x_norm)
            w_q = w + jax.lax.stop_gradient(weight_quant(w) - w)
            return jnp.einsum('bsd,od->bso', x_q, w_q)
        h = bitlinear(x, w_in, g_in)
        up, gate = jnp.split(h, 2, axis=-1)
        y = jax.nn.silu(gate) * up
        return bitlinear(y, w_out, g_out)

    def _L1_attn_ref(hidden_states, Wq, Wk, Wv, Wo):
        import jax, jax.numpy as jnp
        import numpy as np
        N_EMBD = 192
        N_HEAD = 12
        N_KV_HEAD = 4
        NUM_KV_HEADS = N_HEAD // N_KV_HEAD
        HEAD_DIM = N_EMBD // N_HEAD
        BLOCK_SIZE = 256
        SCALE = (HEAD_DIM * N_KV_HEAD / N_HEAD) ** (-0.5)

        def _rotary_cos_sin(T, d, dtype):
            inv_freq = 1.0 / 10000.0 ** (jnp.arange(0, d, 2, dtype=jnp.float32) / d)
            t = jnp.arange(T, dtype=jnp.float32)
            freqs = jnp.outer(t, inv_freq)
            return (jnp.cos(freqs).astype(dtype)[None, None], jnp.sin(freqs).astype(dtype)[None, None])

        def _apply_rotary(x):
            T, d = (x.shape[2], x.shape[3])
            cos, sin = _rotary_cos_sin(T, d, x.dtype)
            x1, x2 = (x[..., :d // 2], x[..., d // 2:])
            return jnp.concatenate([x1 * cos - x2 * sin, x1 * sin + x2 * cos], axis=-1)
        b, T, _ = hidden_states.shape
        q = (hidden_states @ Wq.T).reshape(b, T, N_HEAD, HEAD_DIM).transpose(0, 2, 1, 3)
        k = (hidden_states @ Wk.T).reshape(b, T, NUM_KV_HEADS, HEAD_DIM).transpose(0, 2, 1, 3)
        v = (hidden_states @ Wv.T).reshape(b, T, NUM_KV_HEADS, HEAD_DIM).transpose(0, 2, 1, 3)
        k = jnp.repeat(k, N_KV_HEAD, axis=1)
        v = jnp.repeat(v, N_KV_HEAD, axis=1)
        q = _apply_rotary(q)
        k = _apply_rotary(k)
        W = BLOCK_SIZE
        i = jnp.arange(T)[:, None]
        j = jnp.arange(T)[None, :]
        start = jnp.clip(i - W // 2, 0, T - W)
        mask = (j >= start) & (j < start + W)
        scores = jnp.einsum('bhqd,bhkd->bhqk', q, k) * SCALE
        scores = jnp.where(mask[None, None], scores, jnp.finfo(scores.dtype).min)
        attn = jax.nn.softmax(scores, axis=-1)
        out = jnp.einsum('bhqk,bhkd->bhqd', attn, v)
        out = out.transpose(0, 2, 1, 3).reshape(b, T, N_EMBD)
        return out @ Wo.T

    def _L1_ffn_ref(hidden_states, router_w, router_b, w1, w2, w3):
        import jax, jax.numpy as jnp
        import numpy as np
        S, B, DIM = (256, 4, 192)
        N_EXPERTS = 8
        HID = 512
        s, b, h = hidden_states.shape
        route = jax.nn.softmax(hidden_states @ router_w + router_b, axis=2)
        max_prob = jnp.max(route, axis=2).reshape(-1, 1)
        max_ind = jnp.argmax(route, axis=2).reshape(-1)
        x = hidden_states.reshape(-1, h)
        out = jnp.zeros_like(x)
        for e in range(N_EXPERTS):
            mask = (max_ind == e)[:, None]
            xe = jnp.where(mask, x, 0.0)
            oe = jax.nn.silu(xe @ w1[e]) * (xe @ w2[e]) @ w3[e]
            out = out + jnp.where(mask, oe, 0.0)
        out = out.astype(jnp.bfloat16) * max_prob
        return out.reshape(s, b, h)
    h = _L0_tok_ref(x, L0_tok_w_dw, L0_tok_b_dw, L0_tok_w_pw, L0_tok_b_pw, L0_tok_gamma, L0_tok_beta)
    h = h + _L0_attn_ref(_layernorm(h, axis=-1), L0_attn_Wq, L0_attn_Wk, L0_attn_Wv, L0_attn_Wrk, L0_attn_r_w_bias, L0_attn_r_r_bias, L0_attn_Wo, L0_attn_bo)
    h = h + _L0_ffn_ref(_layernorm(h, axis=-1), L0_ffn_w_in, L0_ffn_g_in, L0_ffn_w_out, L0_ffn_g_out)
    h = h + _L1_attn_ref(_layernorm(h, axis=-1), L1_attn_Wq, L1_attn_Wk, L1_attn_Wv, L1_attn_Wo)
    h = h + _L1_ffn_ref(_layernorm(h, axis=-1), L1_ffn_router_w, L1_ffn_router_b, L1_ffn_w1, L1_ffn_w2, L1_ffn_w3)
    return h

_drawn_inputs = setup_inputs


def setup_inputs(seed=0):
    import zlib

    import numpy as np

    out = dict(_drawn_inputs(seed))
    spreads = {'L0_tok_gamma': (1.0, 0.2),
     'L0_tok_beta': (0.0, 0.1),
     'L0_attn_bo': (0.0, 0.1),
     'L0_ffn_g_in': (1.0, 0.6),
     'L0_ffn_g_out': (1.0, 0.6),
     'L1_ffn_router_b': (0.0, 0.8)}
    factors = {'L0_attn_Wq': 8.0,
     'L0_attn_Wk': 8.0,
     'L0_attn_Wv': 2.944,
     'L0_attn_Wrk': 8.0,
     'L0_attn_r_w_bias': 8.0,
     'L0_attn_r_r_bias': 8.0,
     'L0_attn_Wo': 2.859,
     'L0_ffn_w_in': 8.0,
     'L0_ffn_w_out': 8.0,
     'L1_attn_Wq': 8.0,
     'L1_attn_Wk': 8.0,
     'L1_attn_Wv': 4.832,
     'L1_attn_Wo': 4.371,
     'L1_ffn_router_w': 8.0,
     'L1_ffn_w1': 8.0,
     'L1_ffn_w2': 8.0,
     'L1_ffn_w3': 8.0}
    for name, (base, spread) in spreads.items():
        noise = np.random.default_rng([zlib.crc32(name.encode()), seed]).standard_normal(out[name].shape)
        drawn = base * np.exp(spread * noise) if base else spread * noise
        out[name] = jnp.asarray(drawn.astype(out[name].dtype))
    for name, factor in factors.items():
        out[name] = (out[name] * factor).astype(out[name].dtype)
    return out
```

```python
import concourse.bass as bass
from concourse import mybir
from contextlib import ExitStack
import numpy as np

FP32 = mybir.dt.float32
BF16 = mybir.dt.bfloat16
I32 = mybir.dt.int32
ALU = mybir.AluOpType
ACT = mybir.ActivationFunctionType
AX = mybir.AxisListType

NB, SEQ, D = 64, 125, 192
TAPS = 7
T = SEQ // 2
TP = 64
P = 128
TILES = NB // 2
PEELED = 5
E_PEELED = 3
HALO = TAPS // 2
XW = SEQ + 2 * HALO
PAIRS = 2 * T
H0, DK, DV, NF = 8, 64, 96, 32
HP = H0 // 2
REL = 2 * T - 1
RW = HP * REL
HID0 = 512
H1, KV1, HD = 12, 3, 16
REP = H1 // KV1
QKV1 = (H1 + 2 * KV1) * HD
NE, HID1 = 8, 512
KT = 2
KB = D - P
CAP = 4096
MAX_TILES = TILES + NE
MAGIC = 1.5 * 2.0 ** 23
EPS = 1e-5
EPS_RMS = 1e-6
SCALE1 = (HD * REP / H1) ** -0.5


def first(m):
    return isinstance(m, int) and m == 0


def after_previous(eng, sem, count):
    if not (isinstance(count, int) and count <= 0):
        eng.wait_ge(sem, count)


class Chain:

    def __init__(self, eng, sem):
        self.eng, self.sem, self.n, self.per_tile, self.base = eng, sem, 0, None, 0

    def tile(self, m):
        if self.per_tile is None and self.n:
            self.per_tile = self.n
        self.base = 0 if first(m) else m * self.per_tile
        self.n = 0

    def mark(self, ins):
        ins.then_inc(self.sem, 1)
        self.n += 1

    def wait(self, back=0):
        self.eng.wait_ge(self.sem, self.base + self.n - back)

    def link(self, ins):
        self.mark(ins)
        self.wait()


def audio_tower(nc, x, taps, w_pw, b_pw, dft, dft_seq, gamma, beta,
                wq0, wk0, wv0, wo0, rk_feat, wrk, bias_q, w_in, g_in, w_out, g_out,
                wqkv1, wo1, rope, blocks, ident_in, router_w, router_b, w1, w2, w3, tri, real, prefer, region, steps, out):
    LG, RK, TT = QKV1 + 32, 2 * P, 2 * P + 16
    routed = nc.dram_tensor("routed", ((NE + 1) * CAP, D), FP32).ap()
    answered = nc.dram_tensor("answered", (MAX_TILES * P, D), BF16).ap()
    rel_dram = nc.dram_tensor("rel_scores", (2 * TP, 2 * RW), FP32).ap()
    ctx = ExitStack()
    loop_mem = ExitStack()
    with ctx:
        def sb(name, shape, dt=FP32, mem=None):
            return (mem or ctx).enter_context(nc.sbuf_tensor(name, shape, dt))

        def sem(name):
            return ctx.enter_context(nc.semaphore(name))

        ident = sb("ident", [P, P])
        resid = sb("resid", [P, TILES, D])
        slots = sb("slots", [P, TILES])
        max_prob = sb("max_prob", [P, TILES])
        filled = sb("filled", [P, NE + 1])
        c_region = sb("c_region", [P, NE + 1])
        c_steps = sb("c_steps", [P, MAX_TILES])
        zeros = sb("zeros", [P, D])
        zeros16 = sb("zeros16", [P, D], BF16)
        w3_sb = sb("w3_sb", [P, NE, HID1 // P, D])
        pool_spare = sb("pool_spare", [P, 1])
        half = sb("half", [P, 1])

        def lp(name, shape, dt=FP32):
            return sb(name, shape, dt, loop_mem)

        c_taps = lp("c_taps", [P, 2, TAPS + 1])
        c_bpw = lp("c_bpw", [P, 2])
        c_wpw = lp("c_wpw", [P, 3, D])
        c_dft = lp("c_dft", [P, KT, 2 * D])
        c_dft_seq = lp("c_dft_seq", [P, 2, P])
        c_gamma = lp("c_gamma", [P, D])
        c_beta = lp("c_beta", [P, D])
        x_tok = lp("x_tok", [SEQ, 2, D])
        xT_lo = lp("xT_lo", [P, 2, XW])
        xT_hi = lp("xT_hi", [P, XW])
        conv_lo = lp("conv_lo", [P, 2, PAIRS])
        conv_hi = lp("conv_hi", [P, PAIRS])
        pooled = lp("pooled", [P, KT, 2, T])
        hT = lp("hT", [P, KT, 2, TP])
        z_sb = lp("z_sb", [P, 2 * D])
        c_wq0 = lp("c_wq0", [P, KT, H0 * DK])
        c_wk0 = lp("c_wk0", [P, KT, H0 * DK])
        c_wv0 = lp("c_wv0", [P, KT, H0 * DV])
        c_wo0 = lp("c_wo0", [DV + 1, H0, D])
        c_feat = lp("c_feat", [NF, REL])
        c_wrk = lp("c_wrk", [NF, H0 * DK])
        c_bias_q = lp("c_bias_q", [P, 2, HP])
        rkBD = lp("rkBD", [P, HP, 2, REL])
        a_in = lp("a_in", [P, D])
        res_a, res_f, res_b, res_m = (lp(f"res_{k}", [P, D]) for k in "afbm")
        a_xT = lp("a_xT", [P, KT, P])
        qr = lp("qr", [P, HP, P])
        qBD = lp("qBD", [P, HP, 2, 2, TP])
        kT0 = lp("kT0", [P, HP, P])
        v0 = lp("v0", [P, H0 * DV])
        rel_tok = lp("rel_tok", [P, 2, REL, HP])
        rel_skew = lp("rel_skew", [P, 2, T, HP])
        s0 = lp("s0", [P, H0, T])
        p0 = lp("p0", [P, HP, 2, TP])
        pT0 = lp("pT0", [P, H0, 2, TP])
        oT0 = lp("oT0", [DV + 1, H0, P])
        c_win_f = lp("c_win_f", [P, KT, 2 * HID0])
        c_wout_f = lp("c_wout_f", [P, HID0 // P, D])
        c_win = lp("c_win", [P, KT, 2 * HID0], BF16)
        c_wout = lp("c_wout", [P, HID0 // P, D], BF16)
        c_gin = lp("c_gin", [P, D])
        c_gout = lp("c_gout", [P, HID0])
        ident16 = lp("ident16", [P, P], BF16)
        wsum = lp("wsum", [P, 2])
        wsc = lp("wsc", [P, 4])
        f_in = lp("f_in", [P, D])
        f_sq = lp("f_sq", [P, HID0])
        f_x = lp("f_x", [P, D])
        f_xq = lp("f_xq", [P, D], BF16)
        f_xqT = lp("f_xqT", [P, KT, P], BF16)
        f_tanh = lp("f_tanh", [P, HID0])
        f_gate = lp("f_gate", [P, HID0])
        f_y = lp("f_y", [P, HID0])
        f_yq = lp("f_yq", [P, HID0], BF16)
        f_yqT = lp("f_yqT", [P, HID0 // P, P], BF16)
        c_wqkv1 = lp("c_wqkv1", [P, KT, QKV1])
        c_wo1 = lp("c_wo1", [P, KT, D])
        c_rope = lp("c_rope", [P, 2, HD])
        c_blocks = lp("c_blocks", [P, 2 * REP])
        b_in = lp("b_in", [P, D])
        b_xT = lp("b_xT", [P, KT, P])
        rot_c = lp("rot_c", [P, H1 + KV1, HD])
        rot_s = lp("rot_s", [P, H1 + KV1, HD])
        q_rot = lp("q_rot", [P, H1, HD])
        k_rep = lp("k_rep", [P, KV1, REP, HD])
        vBD = lp("vBD", [P, 2, KV1, 2, HD])
        qT1 = lp("qT1", [P, KT, P])
        kBD_lo = lp("kBD_lo", [P, 2 * REP, P])
        kBD_hi = lp("kBD_hi", [P, REP, P])
        s1 = lp("s1", [P, H1, T])
        p1 = lp("p1", [P, H1, TP])
        pT1 = lp("pT1", [P, H1 // 2, P])
        o1 = lp("o1", [P, H1, HD])
        oT1 = lp("oT1", [P, KT, P])
        moe_now = lp("moe_now", [P, D])
        r_xT = lp("r_xT", [P, KT, P])
        lg, r_exp, best = lp("lg", [P, NE]), lp("r_exp", [P, NE]), lp("best", [P, NE])
        neg_max, exp_sum, best_one, slot_f = (lp(k, [P, 1]) for k in ("neg_max", "exp_sum", "best_one", "slot_f"))
        slot_now = lp("slot_now", [P, 1], I32)
        chosen = lp("chosen", [P, NE + 1])
        place, place_one = lp("place", [P, NE + 1]), lp("place_one", [P, NE + 1])
        c_tri = lp("c_tri", [P, P])
        c_prefer = lp("c_prefer", [P, NE])
        c_real = lp("c_real", [P, 2])
        c_rw = lp("c_rw", [P, KT, NE])
        c_rb = lp("c_rb", [P, NE])
        spare = lp("spare", [1, 1])
        ones = lp("ones", [P, P])
        st = {k: lp(f"stats_{k}", [P, 6]) for k in ("t1", "t2", "a", "f", "b")}
        mv = {k: lp(f"meanvar_{k}", [P, 2]) for k in ("t1", "t2", "a", "f", "b")}
        var = {k: lp(f"var_{k}", [P, 1]) for k in ("t1", "t2", "a", "f", "b", "x", "y")}
        rstd = {k: lp(f"rstd_{k}", [P, 1]) for k in ("t1", "t2", "a", "f", "b", "x", "y")}
        ssq = {k: lp(f"ssq_{k}", [P, 1]) for k in ("x", "y")}
        amax = {k: lp(f"amax_{k}", [P, 1]) for k in ("x", "y")}
        qsc = {k: lp(f"qscale_{k}", [P, 2]) for k in ("x", "y")}
        dq = {k: lp(f"dequant_{k}", [P, 3]) for k in ("x", "y")}
        max0 = lp("max0", [P, H0])
        sum0 = lp("sum0", [P, H0])
        inv0 = lp("inv0", [P, H0])
        max1 = lp("max1", [P, H1])
        sum1 = lp("sum1", [P, H1])
        inv1 = lp("inv1", [P, H1])

        def bank(name):
            return ctx.enter_context(nc.psum_tensor(name, [P, 512], FP32))
        pt, pa0, pa1, pa2, pf0, pf1, pb0, pb1 = (bank(f"bank_{k}") for k in (
            "t", "a0", "a1", "a2", "f0", "f1", "b0", "b1"))

        w_t, w_a, w_f, w_b = sem("weights_t"), sem("weights_a"), sem("weights_f"), sem("weights_b")
        cleared, cleared_dve, half_set = sem("cleared"), sem("cleared_dve"), sem("half_set")
        rk_done, rk_stored = sem("rk_done"), sem("rk_stored")
        wabs, wtotal, wtern = sem("wabs"), sem("wtotal"), sem("wtern")
        setup_dve, w_e, answers_cleared = sem("setup_dve"), sem("weights_e"), sem("answers_cleared")
        x_loaded, t_xpose, t_xT, t_conv, t_pw, t_pooled, t_h, t_z, t_zs, t_y = (sem(f"t_{k}") for k in (
            "x_loaded", "transposed", "xT_ready", "conv_done", "pointwise_done", "pooled", "h_ready",
            "z_done", "z_ready", "y_done"))
        t_yread, t_out = sem("t_y_read"), sem("t_out_ready")
        var_ready = {k: sem(f"var_ready_{k}") for k in var}
        rstd_ready = {k: sem(f"rstd_ready_{k}") for k in var}
        (a_xpose, a_xTr, a_q, a_k, a_v1, a_v2, a_qrr, a_qbd, a_kr, a_v1r, a_v2r, a_r, a_rs, a_wr, a_rel, a_s,
         a_shift, a_exp, a_p, a_pt, a_ptr, a_o, a_or, a_y, a_yread, a_out) = (sem(f"a_{k}") for k in (
            "transposed", "xT_ready", "q_done", "k_done", "v_lo_done", "v_hi_done", "qr_ready", "q_blocks_ready",
            "k_ready", "v_lo_ready", "v_hi_ready", "rel_done", "rel_ready", "rel_written", "rel_skewed",
            "scores_done", "shifted", "exp_ready", "probs_ready", "probs_transposed", "pT_ready", "heads_done",
            "heads_ready", "y_done", "y_read", "out_ready"))
        (f_ssx, f_xqr, f_xpose, f_xTr, f_up, f_gt, f_tanhr, f_yr, f_ssy, f_yqr, f_ypose, f_yTr, f_o, f_out) = (
            sem(f"f_{k}") for k in ("x_squares", "x_quantised", "x_transposed", "xT_ready", "up_done", "gate_done",
                                    "tanh_ready", "y_ready", "y_squares", "y_quantised", "y_transposed",
                                    "yT_ready", "down_done", "out_ready"))
        (b_xpose, b_xTr, b_qkv, b_vr, b_rot, b_qpose, b_kpose, b_qTr, b_kBDr, b_s, b_shift, b_exp, b_sread, b_pt, b_ptr,
         b_o, b_or, b_opose, b_oTr, b_y, b_yread, b_out) = (sem(f"b_{k}") for k in (
            "transposed", "xT_ready", "qkv_done", "v_ready", "rotated", "q_transposed", "k_transposed", "qT_ready",
            "k_blocks_ready", "scores_done", "shifted", "exp_ready", "sums_ready", "probs_transposed", "pT_ready",
            "heads_done", "heads_ready", "heads_transposed", "oT_ready", "y_done", "y_read", "out_ready"))
        (r_xpose, r_xTr, r_l, r_max, r_sum, r_onehot, r_ranked, r_read, r_slot, r_scattered) = (sem(f"r_{k}") for k in (
            "transposed", "xT_ready", "logits_done", "max_ready", "exp_sum_ready", "chosen", "ranks_done", "ranks_read",
            "slots_ready", "scattered"))
        chains = {k: sem(f"chain_{k}") for k in ("dve_t", "dve_a", "dve_f", "dve_b", "dve_r", "dve_m")}

        loop_mem.close()
        w1_sb = sb("w1_sb", [P, NE, KT, HID1])
        w2_sb = sb("w2_sb", [P, NE, KT, HID1])
        e_tok = sb("e_tok", [P, D])
        e_xT = sb("e_xT", [P, KT, P])
        e_tanh = sb("e_tanh", [P, HID1])
        e_gate = sb("e_gate", [P, HID1])
        e_y = sb("e_y", [P, HID1])
        e_yT = sb("e_yT", [P, HID1 // P, P])
        e_out = sb("e_out", [P, D], BF16)
        experts_said = sb("experts_said", [P, TILES, D], BF16)
        EXPERT, FIRST_ROW, PAD_ROW, STEPS = 0, MAX_TILES, 2 * MAX_TILES, 2 * MAX_TILES + NE
        plan = sb("plan", [P, STEPS + 3], I32)
        plan_f = sb("plan_f", [P, STEPS + 3])
        tiles_of = sb("tiles_of", [P, NE])
        tiles_before = sb("tiles_before", [P, NE + 1])
        jump = sb("jump", [P, NE])
        reached = sb("reached", [P, MAX_TILES])
        slot_past = sb("slot_past", [P, TILES])
        answer_at_f = sb("answer_at_f", [P, TILES])
        answer_at = sb("answer_at", [P, TILES], I32)
        e_spare = sb("e_spare", [1, 1])
        weighted = sb("weighted", [P, TILES // 4, D])
        planned, pads_written, located = sem("planned"), sem("pads_written"), sem("answers_located")
        (e_loaded, e_xpose, e_xTr, e_g, e_u, e_tanhr, e_yr, e_ypose, e_yTr, e_o, e_or, e_stored, all_stored) = (sem(f"e_{k}") for k in (
            "x_loaded", "transposed", "xT_ready", "gate_done", "up_done", "tanh_ready", "y_ready", "y_transposed",
            "yT_ready", "down_done", "out_ready", "stored", "all_stored"))
        scaled, finished, stored = (sem(k) for k in ("scaled", "finished", "stored"))
        GROUPS, GT = 4, TILES // 4
        gathered = [sem(f"gathered_{g}") for g in range(GROUPS)]

        def staggered(eng, stages):
            lag = {"x": 0, "g": 1, "y": 2}
            eng.wait_ge(planned, 1)
            total, last, last_but_one = (
                eng.value_load(plan[0:1, STEPS + k:STEPS + k + 1], min_val=TILES - 1 - k, max_val=MAX_TILES - k) for k in range(3))

            def body(steps):
                for name, stage in stages:
                    if name in steps:
                        stage(steps[name])
            for j in range(E_PEELED):
                body({name: j - late for name, late in lag.items() if j >= late})
            with eng.Fori(E_PEELED, total) as j:
                body({name: j - late for name, late in lag.items()})
            body({"g": last, "y": last_but_one})
            body({"y": last})
            return total

        block = ctx.enter_context(nc.Block())
        LOADS_T, LOADS_A, LOADS_F, LOADS_B = 9 * 16, 7 * 16, 5 * 16, 10 * 16

        def overlapped(eng, stages):
            lag = {"t": 0, "a": 1, "f": 2, "b": 3, "r": 4}

            def body(n):
                for name, stage in stages:
                    m = n - lag[name]
                    if not isinstance(m, int) or 0 <= m < TILES:
                        stage(m)
            for n in range(PEELED):
                body(n)
            with eng.Fori(PEELED, TILES) as n:
                body(n)
            for n in range(TILES, TILES + 4):
                body(n)

        @block.sync
        def _(sp):
            def load_x(m):
                src = x[bass.ds(sp.snap(2 * m), 2)] if not isinstance(m, int) else x[2 * m:2 * m + 2]
                if not first(m):
                    sp.wait_ge(t_xpose, m)
                sp.dma_start(x_tok[:, :, :], src.rearrange("b s c -> s b c")).then_inc(x_loaded, 16)

            sp.dma_start(ident[:, :], ident_in).then_inc(w_t, 16)
            load_x(0)
            sp.dma_start(c_taps[:, :, :], taps).then_inc(w_t, 16)
            sp.dma_start(c_bpw[:, :], b_pw).then_inc(w_t, 16)
            sp.dma_start(c_wpw[:, :, :], w_pw).then_inc(w_t, 16)
            sp.dma_start(c_dft[:, :, :], dft).then_inc(w_t, 16)
            sp.dma_start(c_dft_seq[:, :, :], dft_seq).then_inc(w_t, 16)
            sp.dma_start(c_gamma[:, :], bass.AP(gamma.tensor, 0, [[0, P], [1, D]])).then_inc(w_t, 16)
            sp.dma_start(c_beta[:, :], bass.AP(beta.tensor, 0, [[0, P], [1, D]])).then_inc(w_t, 16)
            sp.dma_start(c_feat[:, :], rk_feat).then_inc(w_t, 16)
            sp.dma_start(c_wrk[:, :], wrk).then_inc(w_a, 16)
            sp.dma_start(c_bias_q[:, :, :], bias_q).then_inc(w_a, 16)
            sp.dma_start(c_wq0[:, :, :], wq0).then_inc(w_a, 16)
            sp.dma_start(c_wk0[:, :, :], wk0).then_inc(w_a, 16)
            sp.dma_start(c_wv0[:, :, :], wv0).then_inc(w_a, 16)
            sp.dma_start(c_wo0[:, :, :], wo0).then_inc(w_a, 16)
            sp.dma_start(c_rw[:, :, :], router_w).then_inc(w_a, 16)
            sp.dma_start(c_win_f[:, :, :], w_in).then_inc(w_f, 16)
            sp.dma_start(c_wout_f[:, :, :], w_out).then_inc(w_f, 16)
            sp.dma_start(c_gin[:, :], bass.AP(g_in.tensor, 0, [[0, P], [1, D]])).then_inc(w_f, 16)
            sp.dma_start(c_gout[:, :], bass.AP(g_out.tensor, 0, [[0, P], [1, HID0]])).then_inc(w_f, 16)
            sp.dma_start(c_rb[:, :], bass.AP(router_b.tensor, 0, [[0, P], [1, NE]])).then_inc(w_f, 16)
            sp.dma_start(c_wqkv1[:, :, :], wqkv1).then_inc(w_b, 16)
            sp.dma_start(c_wo1[:, :, :], wo1).then_inc(w_b, 16)
            sp.dma_start(c_rope[:, :, :], rope).then_inc(w_b, 16)
            sp.dma_start(c_blocks[:, :], blocks).then_inc(w_b, 16)
            sp.dma_start(w3_sb[:, :, :, :], w3.rearrange("e (k p) d -> p e k d", p=P)).then_inc(w_e, 16)
            sp.wait_ge(cleared, 5)
            sp.dma_start(answered.rearrange("(a p) d -> p a d", p=P),
                         zeros16[:, :].unsqueeze(1).broadcast_to([P, MAX_TILES, D])).then_inc(answers_cleared, 16)
            sp.dma_start(c_tri[:, :], tri).then_inc(w_b, 16)
            sp.dma_start(c_prefer[:, :], prefer).then_inc(w_b, 16)
            sp.dma_start(c_real[:, :], real).then_inc(w_b, 16)
            sp.dma_start(filled[:, :], region).then_inc(w_b, 16)
            sp.dma_start(c_region[:, :], region).then_inc(w_b, 16)
            sp.dma_start(c_steps[:, :], steps).then_inc(w_b, 16)

            def next_x(m):
                load_x(m + 1)

            def skew(m):
                written = 16 * m + 16 if isinstance(m, int) else sp.snap(16 * m + 16)
                used = m if isinstance(m, int) else sp.snap(m)
                after_previous(sp, a_rel, 32 * m)
                sp.wait_ge(a_rs, 2 * m + 2)
                sp.dma_start(rel_dram, rel_tok[:, :, :, :].rearrange("p a r h -> p (a r h)")).then_inc(a_wr, 16)
                sp.wait_ge(a_wr, written)
                if not first(m):
                    sp.wait_ge(a_shift, used)
                for h2 in range(2):
                    sp.dma_start(
                        rel_skew[TP * h2:TP * h2 + TP, :, :, :].rearrange("p b s h -> p b (s h)"),
                        bass.AP(rel_dram.tensor, h2 * RW + (T - 1) * HP,
                                [[2 * RW - HP, TP], [2 * RW * TP, 2], [1, T * HP]])).then_inc(a_rel, 16)

            for n in range(PEELED):
                next_x(n)
                if n >= 1:
                    skew(n - 1)
            with sp.Fori(PEELED, TILES - 1) as n:
                next_x(n)
                skew(n - 1)
            skew(TILES - 2)
            skew(TILES - 1)
            sp.wait_ge(r_scattered, 16 * TILES)
            sp.wait_ge(planned, 1)
            sp.wait_ge(answers_cleared, 16)
            for lo, w, src in ((0, w1_sb, w1), (0, w2_sb, w2)):
                sp.dma_start(w[:, :, 0, :], src[:, 0:P, :].rearrange("e p n -> p e n")).then_inc(w_e, 16)
                sp.dma_start(w[0:KB, :, 1, :], src[:, P:D, :].rearrange("e p n -> p e n")).then_inc(w_e, 16)
            for e in range(NE):
                at = sp.value_load(plan[0:1, PAD_ROW + e:PAD_ROW + e + 1], min_val=0, max_val=NE * CAP)
                sp.dma_start(routed[bass.ds(at, P), :], zeros[:, :]).then_inc(pads_written, 16)
            sp.wait_ge(pads_written, 16 * NE)

            def first_row(j):
                at = plan[0:1, FIRST_ROW + j:FIRST_ROW + j + 1] if isinstance(j, int) else plan[0:1, bass.ds(j + FIRST_ROW, 1)]
                return sp.value_load(at, min_val=0, max_val=NE * CAP)

            def load_rows(j):
                src = routed[bass.ds(first_row(j), P), :]
                if not first(j):
                    sp.wait_ge(e_xpose, j)
                sp.dma_start(e_tok[:, :], src).then_inc(e_loaded, 16)

            def store_rows(j):
                dst = answered[P * j:P * j + P, :] if isinstance(j, int) else answered[bass.ds(sp.snap(P * j), P), :]
                sp.wait_ge(e_or, j + 1)
                sp.dma_start(dst, e_out[:, :]).then_inc(e_stored, 16)
            total_steps = staggered(sp, (("x", load_rows), ("y", store_rows)))
            for g in range(GROUPS):
                sp.wait_ge(finished, g + 1)
                for b in range(2):
                    sp.dma_start(out.rearrange("(m two) t c -> two t m c", two=2)[b][:, g * GT:(g + 1) * GT, :],
                                 resid[b * TP:b * TP + T, g * GT:(g + 1) * GT, :]).then_inc(stored, 16)
            sp.wait_ge(stored, 16 * 2 * GROUPS)

        @block.gpsimd
        def _(pool):
            pool.memset(half[:, :], -0.5).then_inc(half_set, 1)
            for t_ in (xT_lo, xT_hi, hT, rkBD, qBD, p0, a_xT, pT0, f_xqT, vBD, qT1, kBD_hi, p1, oT1, b_xT, r_xT):
                a = t_[tuple(slice(None) for _ in t_.shape)]
                last = pool.memset(a, 0.0)
            last.then_inc(cleared, 1)
            pool.wait_ge(cleared, 1)
            pool.memset(oT0[DV:DV + 1, :, :], 1.0).then_inc(cleared, 1)
            pool.wait_ge(cleared, 2)
            pool.memset(ones[:, :], 1.0).then_inc(cleared, 1)
            pool.wait_ge(cleared, 3)
            pool.memset(zeros[:, :], 0.0).then_inc(cleared, 1)
            pool.wait_ge(cleared, 4)
            pool.memset(zeros16[:, :], 0.0).then_inc(cleared, 1)

            def inv_sqrt(k):
                def stage(m):
                    pool.wait_ge(var_ready[k], m + 1)
                    pool.tensor_tensor(out=rstd[k][:, :], in0=var[k][:, :], in1=half[:, :],
                                       op=ALU.pow).then_inc(rstd_ready[k], 1)
                return stage

            def scatter(m):
                pool.wait_ge(r_slot, m + 1)
                pool.tensor_tensor(out=pool_spare[:, :], in0=half[:, :], in1=half[:, :], op=ALU.add)
                pool.indirect_dma_start(out=routed, out_offset=bass.IndirectOffsetOnAxis(ap=slot_now[:, 0:1], axis=0),
                                        in_=moe_now[:, :], in_offset=None).then_inc(r_scattered, 16)
            overlapped(pool, (("f", inv_sqrt("x")), ("f", inv_sqrt("y")), ("r", scatter), ("t", inv_sqrt("t1")), ("b", inv_sqrt("b")),
                              ("f", inv_sqrt("f")), ("a", inv_sqrt("a")), ("t", inv_sqrt("t2"))))
            pool.wait_ge(located, 1)
            pool.wait_ge(all_stored, 1)
            for m in range(TILES):
                pool.indirect_dma_start(out=experts_said[:, m, :], out_offset=None, in_=answered,
                                        in_offset=bass.IndirectOffsetOnAxis(ap=answer_at[:, m:m + 1], axis=0)).then_inc(gathered[m // GT], 16)

        @block.tensor
        def _(pe):
            def mm(dst, lhsT, rhs, start=True, stop=True):
                return nc.tensor.matmul(dst, lhsT, rhs, start=start, stop=stop)

            def xpose(dst, src, idn=None):
                return nc.tensor.transpose(dst, src, ident[0:src.shape[0], 0:src.shape[0]] if idn is None else idn)

            def xpose_rows(dst, src, sig):
                xpose(dst[:, 0:P], src[:, 0:P])
                xpose(dst[0:KB, P:2 * P], src[:, P:D]).then_inc(sig, 1)

            pe.wait_ge(w_t, LOADS_T)
            pe.wait_ge(w_a, LOADS_A)
            for hp in range(HP):
                last = mm(pa0[:, hp * REL:(hp + 1) * REL], c_wrk[:, hp * P:(hp + 1) * P], c_feat[:, :])
            last.then_inc(rk_done, 1)
            pe.wait_ge(wabs, 2)
            pe.wait_ge(cleared, 3)
            mm(pf0[:, 0:2], ones[:, :], wsum[:, :]).then_inc(wtotal, 1)

            def t_transpose(m):
                pe.wait_ge(x_loaded, 16 * m + 16)
                after_previous(pe, t_yread, m)
                for b in range(2):
                    xpose(pt[:, b * SEQ:(b + 1) * SEQ], x_tok[:, b, 0:P])
                for b in range(2):
                    last = xpose(pt[0:KB, (2 + b) * SEQ:(3 + b) * SEQ], x_tok[:, b, P:D])
                last.then_inc(t_xpose, 1)

            def t_pointwise(m):
                pe.wait_ge(t_conv, m + 1)
                for lo, hi, at in ((0, P, 0), (P, D, 2 * PAIRS)):
                    dst = pt[0:hi - lo, at:at + 2 * PAIRS]
                    mm(dst, c_wpw[:, 0, lo:hi], conv_lo[:, :, :].rearrange("p b s -> p (b s)"), stop=False)
                    mm(dst[:, 0:PAIRS], c_wpw[:, 1, lo:hi], conv_hi[:, :], start=False, stop=False)
                    last = mm(dst[:, PAIRS:2 * PAIRS], c_wpw[:, 2, lo:hi], conv_hi[:, :], start=False)
                last.then_inc(t_pw, 1)

            def t_dft(m):
                pe.wait_ge(t_h, m + 1)
                for kt in range(KT):
                    last = mm(pt[:, 0:2 * D], hT[:, kt, :, :].rearrange("p b s -> p (b s)"), c_dft[:, kt, :],
                              start=kt == 0, stop=kt == KT - 1)
                last.then_inc(t_z, 1)

            def t_dft_seq(m):
                pe.wait_ge(t_zs, m + 1)
                mm(pt[:, 0:D], c_dft_seq[:, 0, :], z_sb[:, 0:D], stop=False)
                mm(pt[:, 0:D], c_dft_seq[:, 1, :], z_sb[:, D:2 * D], start=False).then_inc(t_y, 1)

            def a_transpose(m):
                pe.wait_ge(t_out, m + 1)
                after_previous(pe, a_yread, m)
                xpose_rows(pa2, a_in, a_xpose)

            def a_project(m):
                pe.wait_ge(a_xTr, m + 1)
                for w, dst, sig in ((c_wq0, pa0, a_q), (c_wk0, pa1, a_k)):
                    for hp in range(HP):
                        for kt in range(KT):
                            last = mm(dst[:, hp * P:(hp + 1) * P], w[:, kt, hp * P:(hp + 1) * P], a_xT[:, kt, :],
                                      start=kt == 0, stop=kt == KT - 1)
                    last.then_inc(sig, 1)
                for kt in range(KT):
                    last = mm(pa2[:, :], a_xT[:, kt, :], c_wv0[:, kt, 0:512], start=kt == 0, stop=kt == KT - 1)
                last.then_inc(a_v1, 1)

            def a_relative(m):
                pe.wait_ge(a_v1r, m + 1)
                for kt in range(KT):
                    last = mm(pa2[:, 0:H0 * DV - 512], a_xT[:, kt, :], c_wv0[:, kt, 512:H0 * DV],
                              start=kt == 0, stop=kt == KT - 1)
                last.then_inc(a_v2, 1)
                pe.wait_ge(a_qrr, m + 1)
                pe.wait_ge(a_qbd, m + 1)
                pe.wait_ge(a_kr, m + 1)
                for hp in range(HP):
                    last = mm((pa0, pa1)[hp // 2][:, (hp % 2) * 2 * REL:(hp % 2 + 1) * 2 * REL], qr[:, hp, :],
                              rkBD[:, hp, :, :].rearrange("p a r -> p (a r)"))
                    if hp % 2:
                        last.then_inc(a_r, 1)

            def a_scores(m):
                pe.wait_ge(a_v2r, m + 1)
                for hp in range(HP):
                    for b in range(2):
                        at = (hp * 2 + b) * T
                        last = mm(pa2[:, at:at + T], qBD[:, hp, b, :, :].rearrange("p a t -> p (a t)"),
                                  kT0[:, hp, b * TP:b * TP + T])
                last.then_inc(a_s, 1)

            def a_probs_transpose(m):
                pe.wait_ge(a_p, m + 1)
                for hp in range(HP):
                    last = xpose(pa2[:, hp * P:(hp + 1) * P], p0[:, hp, :, :].rearrange("p b s -> p (b s)"))
                last.then_inc(a_pt, 1)

            def a_values(m):
                pe.wait_ge(a_ptr, m + 1)
                for h in range(H0):
                    last = mm((pa0, pa1)[h // 4][0:DV, (h % 4) * P:(h % 4 + 1) * P], v0[:, h * DV:(h + 1) * DV],
                              pT0[:, h, :, :].rearrange("p b t -> p (b t)"))
                    if h % 4 == 3:
                        last.then_inc(a_o, 1)

            def a_output(m):
                pe.wait_ge(a_or, 2 * m + 2)
                for h in range(H0):
                    k = DV + 1 if h == 0 else DV
                    last = mm(pa2[:, 0:D], oT0[0:k, h, :], c_wo0[0:k, h, :], start=h == 0, stop=h == H0 - 1)
                last.then_inc(a_y, 1)

            def f_transpose_x(m):
                pe.wait_ge(f_xqr, m + 1)
                pe_free_f(m)
                d = pf0[:, :].bitcast(BF16)
                xpose(d[:, 0:P], f_xq[:, 0:P], ident16[:, :])
                xpose(d[0:KB, P:2 * P], f_xq[:, P:D], ident16[:, :]).then_inc(f_xpose, 1)

            def pe_free_f(m):
                after_previous(pe, f_out, m)

            def f_up_gate(m):
                pe.wait_ge(f_xTr, m + 1)
                for dst, at, sig in ((pf0, 0, f_up), (pf1, HID0, f_gt)):
                    for kt in range(KT):
                        last = mm(dst[:, :], f_xqT[:, kt, :], c_win[:, kt, at:at + HID0], start=kt == 0, stop=kt == KT - 1)
                    last.then_inc(sig, 1)

            def f_transpose_y(m):
                pe.wait_ge(f_yqr, m + 1)
                d = pf0[:, :].bitcast(BF16)
                for j in range(HID0 // P):
                    last = xpose(d[:, j * P:(j + 1) * P], f_yq[:, j * P:(j + 1) * P], ident16[:, :])
                last.then_inc(f_ypose, 1)

            def f_down(m):
                pe.wait_ge(f_yTr, m + 1)
                for j in range(HID0 // P):
                    last = mm(pf1[:, 0:D], f_yqT[:, j, :], c_wout[:, j, :], start=j == 0, stop=j == HID0 // P - 1)
                last.then_inc(f_o, 1)

            def b_transpose(m):
                pe.wait_ge(f_out, m + 1)
                after_previous(pe, b_yread, m)
                xpose_rows(pb0, b_in, b_xpose)

            def b_project(m):
                pe.wait_ge(b_xTr, m + 1)
                for kt in range(KT):
                    last = mm(pb0[:, 0:QKV1], b_xT[:, kt, :], c_wqkv1[:, kt, :], start=kt == 0, stop=kt == KT - 1)
                last.then_inc(b_qkv, 1)

            def b_transpose_qk(m):
                pe.wait_ge(b_rot, m + 1)
                k = k_rep[:, :, :, :].rearrange("p g r d -> p (g r d)")
                xpose_rows(pb0, q_rot[:, :, :].rearrange("p h d -> p (h d)"), b_qpose)
                xpose_rows(pb1, k, b_kpose)

            def b_scores(m):
                pe.wait_ge(b_qTr, m + 1)
                pe.wait_ge(b_kBDr, m + 1)
                if not first(m):
                    pe.wait_ge(r_read, m)
                for b in range(2):
                    rows = slice(b * TP, (b + 1) * TP)
                    for dst, kt, kbd, n in ((pb0, 0, kBD_lo, 2 * REP), (pb1, 1, kBD_hi, REP)):
                        last = mm(dst[rows, 0:n * T].rearrange("p (h s) -> p h s", h=n), qT1[:, kt, rows],
                                  kbd[:, :, b * TP:b * TP + T])
                last.then_inc(b_s, 1)

            def b_probs_transpose(m):
                pe.wait_ge(b_exp, m + 1)
                for j in range(H1 // 2):
                    last = xpose((pb0, pb1)[j // 4][:, (j % 4) * P:(j % 4 + 1) * P],
                                 p1[:, 2 * j:2 * j + 2, :].rearrange("p h s -> p (h s)"))
                last.then_inc(b_pt, 1)

            def b_values(m):
                pe.wait_ge(b_ptr, m + 1)
                for b in range(2):
                    rows = slice(b * TP, (b + 1) * TP)
                    for j in range(H1 // 2):
                        last = mm(pb0[rows, j * 2 * HD:(j + 1) * 2 * HD], pT1[:, j, rows],
                                  vBD[:, b, j // 2, :, :].rearrange("p a d -> p (a d)"))
                last.then_inc(b_o, 1)

            def b_transpose_o(m):
                pe.wait_ge(b_or, m + 1)
                xpose_rows(pb1, o1[:, :, :].rearrange("p h d -> p (h d)"), b_opose)

            def b_output(m):
                pe.wait_ge(b_oTr, m + 1)
                for kt in range(KT):
                    last = mm(pb0[:, 0:D], oT1[:, kt, :], c_wo1[:, kt, :], start=kt == 0, stop=kt == KT - 1)
                last.then_inc(b_y, 1)

            def r_transpose(m):
                pe.wait_ge(b_out, m + 1)
                xpose_rows(pb1, moe_now, r_xpose)

            def beside_b(m):
                return not isinstance(m, int) or m < TILES - 1

            def r_route(m):
                pe.wait_ge(r_xTr, m + 1)
                if beside_b(m):
                    pe.wait_ge(b_xTr, m + 2)
                for kt in range(KT):
                    last = mm(pb0[:, LG:LG + NE], r_xT[:, kt, :], c_rw[:, kt, :], start=kt == 0, stop=kt == KT - 1)
                last.then_inc(r_l, 1)

            def r_rank(m):
                pe.wait_ge(r_onehot, m + 1)
                if beside_b(m):
                    pe.wait_ge(b_qTr, m + 2)
                mm(pb0[:, RK:RK + NE + 1], c_tri[:, :], chosen[:, :])
                mm(pb0[:, TT:TT + NE + 1], ones[:, :], chosen[:, :]).then_inc(r_ranked, 1)

            pe.wait_ge(rk_stored, 1)
            pe.wait_ge(wtern, 1)
            pe.wait_ge(w_b, LOADS_B)
            overlapped(pe, (
                ("b", b_transpose), ("r", r_transpose), ("a", a_transpose), ("t", t_transpose),
                ("r", r_route), ("b", b_project), ("a", a_project), ("f", f_transpose_x),
                ("b", b_transpose_qk), ("a", a_relative), ("r", r_rank), ("t", t_pointwise),
                ("b", b_scores), ("a", a_scores), ("f", f_up_gate), ("t", t_dft),
                ("b", b_probs_transpose), ("a", a_probs_transpose),
                ("b", b_values), ("a", a_values), ("f", f_transpose_y), ("t", t_dft_seq),
                ("b", b_transpose_o), ("a", a_output), ("b", b_output), ("f", f_down)))
            def expert(j):
                at = plan[0:1, j:j + 1] if isinstance(j, int) else plan[0:1, bass.ds(j, 1)]
                return pe.value_load(at, min_val=0, max_val=NE - 1)

            def weights(w, e, kt, rows=P):
                return w[0:rows, bass.ds(e, 1), kt, :].rearrange("p a n -> p (a n)")

            def e_transpose(j):
                pe.wait_ge(e_loaded, 16 * j + 16)
                after_previous(pe, e_xTr, j)
                xpose_rows(pt, e_tok, e_xpose)

            def e_gate_up(j):
                e = expert(j)
                pe.wait_ge(e_xTr, j + 1)
                after_previous(pe, e_yr, j)
                for w, dst, sig in ((w1_sb, pa0, e_g), (w2_sb, pa1, e_u)):
                    mm(dst[:, :], e_xT[:, 0, :], weights(w, e, 0), stop=False)
                    mm(dst[:, :], e_xT[0:KB, 1, :], weights(w, e, 1, KB), start=False).then_inc(sig, 1)

            def e_transpose_y(j):
                pe.wait_ge(e_yr, j + 1)
                for k in range(HID1 // P):
                    last = xpose(pb0[:, k * P:(k + 1) * P], e_y[:, k * P:(k + 1) * P])
                last.then_inc(e_ypose, 1)

            def e_down(j):
                e = expert(j)
                pe.wait_ge(e_yTr, j + 1)
                after_previous(pe, e_or, j)
                for k in range(HID1 // P):
                    last = mm(pb1[:, 0:D], e_yT[:, k, :], weights(w3_sb, e, k), start=k == 0, stop=k == HID1 // P - 1)
                last.then_inc(e_o, 1)

            pe.wait_ge(w_e, 16 * 5)
            staggered(pe, (("y", e_transpose_y), ("g", e_gate_up), ("x", e_transpose), ("y", e_down)))

        @block.scalar
        def _(act):
            def copy(dst, src):
                return nc.scalar.activation(dst, src, ACT.Copy)

            def copy_rows(dst, src, sig):
                copy(dst[:, 0, :], src[:, 0:P])
                copy(dst[0:KB, 1, :], src[0:KB, P:2 * P]).then_inc(sig, 1)

            act.wait_ge(rk_done, 1)
            act.wait_ge(cleared, 3)
            rk = pa0[:, 0:HP * REL].rearrange("p (h r) -> p h r", h=HP)
            copy(rkBD[0:TP, :, 0, :], rk[0:TP])
            copy(rkBD[TP:P, :, 1, :], rk[TP:P]).then_inc(rk_stored, 1)
            act.wait_ge(w_f, LOADS_F)
            w = c_win_f[:, :, :].rearrange("p a b -> p (a b)")
            nc.scalar.activation(c_win[:, :, :].rearrange("p a b -> p (a b)"), w, ACT.Abs, accum_out=wsum[:, 0:1]).then_inc(wabs, 1)
            w = c_wout_f[:, :, :].rearrange("p a b -> p (a b)")
            nc.scalar.activation(c_wout[:, :, :].rearrange("p a b -> p (a b)"), w, ACT.Abs, accum_out=wsum[:, 1:2]).then_inc(wabs, 1)

            def t_copy_x(m):
                act.wait_ge(t_xpose, m + 1)
                copy(xT_lo[:, :, HALO:HALO + SEQ], pt[:, 0:2 * SEQ].rearrange("p (b s) -> p b s", b=2))
                for b in range(2):
                    last = copy(xT_hi[b * KB:(b + 1) * KB, HALO:HALO + SEQ], pt[0:KB, (2 + b) * SEQ:(3 + b) * SEQ])
                last.then_inc(t_xT, 1)

            def t_relu(m):
                act.wait_ge(t_pooled, m + 1)
                nc.scalar.activation(hT[:, 0, :, 0:T], pooled[:, 0, :, :], ACT.Relu, bias=c_bpw[:, 0:1])
                nc.scalar.activation(hT[0:KB, 1, :, 0:T], pooled[0:KB, 1, :, :], ACT.Relu,
                                     bias=c_bpw[0:KB, 1:2]).then_inc(t_h, 1)

            def t_copy_z(m):
                act.wait_ge(t_z, m + 1)
                copy(z_sb[:, :], pt[:, 0:2 * D]).then_inc(t_zs, 1)

            def a_copy_x(m):
                act.wait_ge(a_xpose, m + 1)
                copy_rows(a_xT, pa2, a_xTr)

            def a_copy_qkv(m):
                act.wait_ge(a_q, m + 1)
                for hp in range(HP):
                    last = nc.scalar.activation(qr[:, hp, :], pa0[:, hp * P:(hp + 1) * P], ACT.Identity,
                                                scale=DK ** -0.5, bias=c_bias_q[:, 1, hp:hp + 1])
                last.then_inc(a_qrr, 1)
                for hp in range(HP):
                    for h2 in range(2):
                        r = slice(h2 * TP, (h2 + 1) * TP)
                        last = nc.scalar.activation(
                            qBD[r, hp, :, h2, :], pa0[r, hp * P:(hp + 1) * P].rearrange("p (b t) -> p b t", b=2),
                            ACT.Identity, scale=DK ** -0.5, bias=c_bias_q[r, 0, hp:hp + 1])
                last.then_inc(a_qbd, 1)
                act.wait_ge(a_k, m + 1)
                copy(kT0[:, :, :].rearrange("p a b -> p (a b)"), pa1[:, :]).then_inc(a_kr, 1)
                act.wait_ge(a_v1, m + 1)
                copy(v0[:, 0:512], pa2[:, :]).then_inc(a_v1r, 1)

            def a_copy_rel(m):
                act.wait_ge(a_v2, m + 1)
                copy(v0[:, 512:H0 * DV], pa2[:, 0:H0 * DV - 512]).then_inc(a_v2r, 1)
                after_previous(act, a_wr, 16 * m)
                for i, src in enumerate((pa0, pa1)):
                    act.wait_ge(a_r, 2 * m + 1 + i)
                    copy(rel_tok[:, :, :, 2 * i:2 * i + 2].rearrange("p a r h -> p h a r"),
                         src[:, 0:4 * REL].rearrange("p (h a r) -> p h a r", h=2, a=2)).then_inc(a_rs, 1)

            def a_expo(m):
                act.wait_ge(a_shift, m + 1)
                nc.scalar.activation(p0[:, :, :, 0:T].rearrange("p h b s -> p (h b) s"), s0[:, :, :],
                                     ACT.Exp).then_inc(a_exp, 1)

            def a_copy_probs(m):
                act.wait_ge(a_pt, m + 1)
                for b in range(2):
                    r = slice(b * TP, (b + 1) * TP)
                    last = copy(pT0[r, :, b, :], pa2[r, :].rearrange("p (h t) -> p h t", h=H0))
                last.then_inc(a_ptr, 1)

            def a_copy_heads(m):
                for i, src in enumerate((pa0, pa1)):
                    act.wait_ge(a_o, 2 * m + 1 + i)
                    copy(oT0[0:DV, 4 * i:4 * i + 4, :].rearrange("p h t -> p (h t)"), src[0:DV, :]).then_inc(a_or, 1)

            def f_square_x(m):
                act.wait_ge(a_out, m + 1)
                nc.scalar.activation(f_sq[:, 0:D], f_in[:, :], ACT.Square, accum_out=ssq["x"][:, :]).then_inc(f_ssx, 1)

            def f_copy_x(m):
                act.wait_ge(f_xpose, m + 1)
                d = pf0[:, :].bitcast(BF16)
                copy_rows(f_xqT, d, f_xTr)

            def f_tanh_gate(m):
                act.wait_ge(f_gt, m + 1)
                nc.scalar.activation(f_tanh[:, :], pf1[:, :], ACT.Tanh, scale=dq["x"][:, 1:2]).then_inc(f_tanhr, 1)

            def f_square_y(m):
                act.wait_ge(f_yr, m + 1)
                nc.scalar.activation(f_sq[:, :], f_y[:, :], ACT.Square, accum_out=ssq["y"][:, :]).then_inc(f_ssy, 1)

            def f_copy_y(m):
                act.wait_ge(f_ypose, m + 1)
                d = pf0[:, :].bitcast(BF16)
                copy(f_yqT[:, :, :].rearrange("p a b -> p (a b)"), d[:, 0:HID0]).then_inc(f_yTr, 1)

            def b_copy_x(m):
                act.wait_ge(b_xpose, m + 1)
                copy_rows(b_xT, pb0, b_xTr)

            def b_copy_v(m):
                act.wait_ge(b_qkv, m + 1)
                v = pb0[:, (H1 + KV1) * HD:QKV1].rearrange("p (g d) -> p g d", g=KV1)
                for b in range(2):
                    for h2 in range(2):
                        last = copy(vBD[h2 * TP:(h2 + 1) * TP, b, :, h2, :], v[b * TP:(b + 1) * TP])
                last.then_inc(b_vr, 1)

            def b_copy_q(m):
                act.wait_ge(b_qpose, m + 1)
                copy_rows(qT1, pb0, b_qTr)

            def b_expo(m):
                act.wait_ge(b_shift, m + 1)
                nc.scalar.activation(p1[:, :, 0:T], s1[:, :, :], ACT.Exp, scale=SCALE1).then_inc(b_exp, 1)

            def b_copy_probs(m):
                act.wait_ge(b_pt, m + 1)
                copy(pT1[:, 0:4, :].rearrange("p a b -> p (a b)"), pb0[:, :])
                copy(pT1[:, 4:6, :].rearrange("p a b -> p (a b)"), pb1[:, 0:2 * P]).then_inc(b_ptr, 1)

            def b_copy_o(m):
                act.wait_ge(b_opose, m + 1)
                copy_rows(oT1, pb1, b_oTr)

            def r_copy_x(m):
                act.wait_ge(r_xpose, m + 1)
                copy_rows(r_xT, pb1, r_xTr)

            def r_expo(m):
                act.wait_ge(r_max, m + 1)
                nc.scalar.activation(r_exp[:, :], lg[:, :], ACT.Exp, bias=neg_max[:, :],
                                     accum_out=exp_sum[:, :]).then_inc(r_sum, 1)

            overlapped(act, (
                ("b", b_copy_x), ("r", r_copy_x), ("a", a_copy_x), ("t", t_copy_x), ("f", f_square_x),
                ("b", b_copy_v), ("a", a_copy_qkv), ("f", f_copy_x),
                ("b", b_copy_q), ("r", r_expo), ("a", a_copy_rel), ("t", t_relu),
                ("b", b_expo), ("a", a_expo), ("f", f_tanh_gate), ("t", t_copy_z), ("f", f_square_y),
                ("b", b_copy_probs), ("a", a_copy_probs), ("a", a_copy_heads), ("f", f_copy_y),
                ("b", b_copy_o)))
            def e_copy_x(j):
                act.wait_ge(e_xpose, j + 1)
                copy_rows(e_xT, pt, e_xTr)

            def e_tanh_gate(j):
                act.wait_ge(e_g, j + 1)
                nc.scalar.activation(e_tanh[:, :], pa0[:, :], ACT.Tanh, scale=0.5).then_inc(e_tanhr, 1)

            def e_copy_y(j):
                act.wait_ge(e_ypose, j + 1)
                copy(e_yT[:, :, :].rearrange("p a b -> p (a b)"), pb0[:, :]).then_inc(e_yTr, 1)
            staggered(act, (("y", e_copy_y), ("g", e_tanh_gate), ("x", e_copy_x)))

        @block.vector
        def _(dve):
            v = nc.vector
            ch = {k: Chain(dve, chains[f"dve_{k}"]) for k in "tafbr"}

            n_setup = [0]

            def setup(ins):
                n_setup[0] += 1
                ins.then_inc(setup_dve, 1)
                dve.wait_ge(setup_dve, n_setup[0])
            dve.wait_ge(w_t, LOADS_T)
            setup(v.tensor_copy(ident16[:, :], ident[:, :]))
            dve.wait_ge(wtotal, 1)
            setup(v.tensor_scalar(wsc[:, 0:1], pf0[:, 0:1], 1.0 / (2 * HID0 * D), EPS, ALU.mult, ALU.max))
            setup(v.tensor_scalar(wsc[:, 1:2], pf0[:, 1:2], 1.0 / (HID0 * D), EPS, ALU.mult, ALU.max))
            setup(v.reciprocal(wsc[:, 2:4], wsc[:, 0:2]))
            for i, (w, q) in enumerate(((c_win_f, c_win), (c_wout_f, c_wout))):
                w, q = (z[:, :, :].rearrange("p a b -> p (a b)") for z in (w, q))
                setup(v.tensor_scalar(w, w, wsc[:, 2 + i:3 + i], MAGIC, ALU.mult, ALU.add))
                setup(v.tensor_scalar(w, w, MAGIC + 1, MAGIC - 1, ALU.min, ALU.max))
                ins = v.tensor_scalar(q, w, MAGIC, None, ALU.subtract)
                setup(ins) if i == 0 else ins.then_inc(wtern, 1)
            dve.wait_ge(wtern, 1)
            dve.wait_ge(cleared, 3)
            dve.wait_ge(w_b, LOADS_B)
            v.tensor_copy(chosen[:, NE:NE + 1], c_real[:, 1:2])

            def moments(c, k, src):
                c.link(v.bn_stats(st[k][:, :], src))
                v.memset(spare[:, :], 0.0)
                c.link(v.bn_aggr(mv[k][:, :], st[k][:, :]))
                v.tensor_scalar(var[k][:, :], mv[k][:, 1:2], EPS, None, ALU.add).then_inc(var_ready[k], 1)

            def normalise(m, k, dst, src):
                dve.wait_ge(rstd_ready[k], m + 1)
                return v.tensor_scalar(dst, src, mv[k][:, 0:1], rstd[k][:, :], ALU.subtract, ALU.mult)

            def row(m):
                return resid[:, m, :] if isinstance(m, int) else resid[:, bass.ds(m, 1), :].rearrange("p a d -> p (a d)")

            def t_convolve(m):
                c = ch["t"]
                c.tile(m)
                dve.wait_ge(t_xT, m + 1)
                c.mark(v.tensor_scalar(conv_lo[:, :, :], xT_lo[:, :, 0:PAIRS], c_taps[:, 0, 0:1],
                                       c_taps[:, 0, TAPS:TAPS + 1], ALU.mult, ALU.add))
                c.mark(v.tensor_scalar(conv_hi[:, :], xT_hi[:, 0:PAIRS], c_taps[:, 1, 0:1],
                                       c_taps[:, 1, TAPS:TAPS + 1], ALU.mult, ALU.add))
                for k in range(1, TAPS):
                    c.wait(back=1)
                    c.mark(v.scalar_tensor_tensor(conv_lo[:, :, :], xT_lo[:, :, k:k + PAIRS], c_taps[:, 0, k:k + 1],
                                                  conv_lo[:, :, :], ALU.mult, ALU.add))
                    c.wait(back=1)
                    ins = v.scalar_tensor_tensor(conv_hi[:, :], xT_hi[:, k:k + PAIRS], c_taps[:, 1, k:k + 1],
                                                 conv_hi[:, :], ALU.mult, ALU.add)
                    if k < TAPS - 1:
                        c.mark(ins)
                    else:
                        ins.then_inc(t_conv, 1)

            def t_pool(m):
                dve.wait_ge(t_pw, m + 1)
                v.tensor_reduce(pooled[:, 0, :, :].rearrange("p b s -> p (b s)"),
                                pt[:, 0:2 * PAIRS].rearrange("p (s two) -> p s two", two=2), axis=AX.X, op=ALU.max)
                v.tensor_reduce(pooled[0:KB, 1, :, :].rearrange("p b s -> p (b s)"),
                                pt[0:KB, 2 * PAIRS:4 * PAIRS].rearrange("p (s two) -> p s two", two=2),
                                axis=AX.X, op=ALU.max).then_inc(t_pooled, 1)

            def t_moments(m):
                dve.wait_ge(t_y, m + 1)
                moments(ch["t"], "t1", pt[:, 0:D])

            def t_norm(m):
                c = ch["t"]
                h = res_a[:, :]
                normalise(m, "t1", h, pt[:, 0:D]).then_inc(t_yread, 1)
                dve.wait_ge(t_yread, m + 1)
                c.link(v.tensor_tensor(h, h, c_gamma[:, :], ALU.mult))
                c.link(v.tensor_tensor(h, h, c_beta[:, :], ALU.add))
                moments(c, "t2", h)

            def t_finish(m):
                after_previous(dve, a_xpose, m)
                normalise(m, "t2", a_in[:, :], res_a[:, :]).then_inc(t_out, 1)

            def a_shift_scores(m):
                c = ch["a"]
                c.tile(m)
                dve.wait_ge(a_s, m + 1)
                dve.wait_ge(a_rel, 32 * m + 32)
                c.link(v.tensor_tensor(s0[:, :, :].rearrange("p (h b) s -> p h b s", h=HP),
                                       pa2[:, 0:H0 * T].rearrange("p (h b s) -> p h b s", h=HP, b=2),
                                       rel_skew[:, :, :, :].rearrange("p b s h -> p h b s"), ALU.add))
                c.link(v.tensor_reduce(max0[:, :], s0[:, :, :], axis=AX.X, op=ALU.max))
                v.tensor_tensor(s0[:, :, :], s0[:, :, :], max0[:, :].unsqueeze(2).broadcast_to([P, H0, T]),
                                ALU.subtract).then_inc(a_shift, 1)

            def a_normalise(m):
                c = ch["a"]
                probs = p0[:, :, :, 0:T].rearrange("p h b s -> p (h b) s")
                dve.wait_ge(a_exp, m + 1)
                c.link(v.tensor_reduce(sum0[:, :], probs, axis=AX.X, op=ALU.add))
                c.link(v.reciprocal(inv0[:, :], sum0[:, :]))
                v.tensor_tensor(probs, probs, inv0[:, :].unsqueeze(2).broadcast_to([P, H0, T]),
                                ALU.mult).then_inc(a_p, 1)

            def a_residual(m):
                c = ch["a"]
                dve.wait_ge(a_y, m + 1)
                v.tensor_tensor(res_f[:, :], res_a[:, :], pa2[:, 0:D], ALU.add).then_inc(a_yread, 1)
                dve.wait_ge(a_yread, m + 1)
                moments(c, "a", res_f[:, :])

            def a_finish(m):
                after_previous(dve, f_ssx, m)
                normalise(m, "a", f_in[:, :], res_f[:, :]).then_inc(a_out, 1)

            def mean_square(m, k, n, ready):
                dve.wait_ge(ready, m + 1)
                v.tensor_scalar(var[k][:, :], ssq[k][:, :], 1.0 / n, EPS_RMS, ALU.mult, ALU.add).then_inc(var_ready[k], 1)

            def quantise(c, m, k, src, gain, work, dst, done):
                dve.wait_ge(rstd_ready[k], m + 1)
                c.link(v.scalar_tensor_tensor(work, src, rstd[k][:, :], gain, ALU.mult, ALU.mult))
                c.link(v.tensor_reduce(amax[k][:, :], work, axis=AX.X, op=ALU.max, apply_absolute_value=True))
                c.link(v.tensor_scalar(amax[k][:, :], amax[k][:, :], EPS, None, ALU.max))
                c.link(v.reciprocal(qsc[k][:, 0:1], amax[k][:, :]))
                c.link(v.tensor_scalar(qsc[k][:, 1:2], qsc[k][:, 0:1], 127.0, None, ALU.mult))
                w = wsc[:, 0:1] if k == "x" else wsc[:, 1:2]
                c.link(v.tensor_scalar(dq[k][:, 0:1], amax[k][:, :], 1.0 / 127.0, w, ALU.mult, ALU.mult))
                c.link(v.tensor_scalar(work, work, qsc[k][:, 1:2], MAGIC, ALU.mult, ALU.add))
                if k == "x":
                    c.link(v.tensor_scalar(dq[k][:, 1:2], dq[k][:, 0:1], 0.5, None, ALU.mult))
                    c.link(v.tensor_scalar(dq[k][:, 2:3], dq[k][:, 1:2], dq[k][:, 0:1], None, ALU.mult))
                v.tensor_scalar(dst, work, MAGIC + 127, MAGIC, ALU.min, ALU.subtract).then_inc(done, 1)

            def f_mean_x(m):
                ch["f"].tile(m)
                mean_square(m, "x", D, f_ssx)

            def f_quantise_x(m):
                quantise(ch["f"], m, "x", f_in[:, :], c_gin[:, :], f_x[:, :], f_xq[:, :], f_xqr)

            def f_silu(m):
                c = ch["f"]
                dve.wait_ge(f_up, m + 1)
                dve.wait_ge(f_tanhr, m + 1)
                c.link(v.scalar_tensor_tensor(f_gate[:, :], f_tanh[:, :], 1.0, pf1[:, :], ALU.add, ALU.mult))
                v.scalar_tensor_tensor(f_y[:, :], f_gate[:, :], dq["x"][:, 2:3], pf0[:, :], ALU.mult,
                                       ALU.mult).then_inc(f_yr, 1)

            def f_mean_y(m):
                mean_square(m, "y", HID0, f_ssy)

            def f_quantise_y(m):
                quantise(ch["f"], m, "y", f_y[:, :], c_gout[:, :], f_gate[:, :], f_yq[:, :], f_yqr)

            def f_residual(m):
                c = ch["f"]
                dve.wait_ge(f_o, m + 1)
                c.link(v.scalar_tensor_tensor(res_b[:, :], pf1[:, 0:D], dq["y"][:, 0:1], res_f[:, :], ALU.mult, ALU.add))
                moments(c, "f", res_b[:, :])

            def f_finish(m):
                after_previous(dve, b_xpose, m)
                normalise(m, "f", b_in[:, :], res_b[:, :]).then_inc(f_out, 1)

            def b_rotate(m):
                c = ch["b"]
                c.tile(m)
                dve.wait_ge(b_vr, m + 1)
                n, hd = H1 + KV1, HD // 2
                qk = pb0[:, 0:n * HD].rearrange("p (h d) -> p h d", h=n)
                c.mark(v.tensor_tensor(rot_c[:, :, :], qk, c_rope[:, 0:1, :].broadcast_to([P, n, HD]), ALU.mult))
                c.mark(v.tensor_tensor(rot_s[:, :, 0:hd], qk[:, :, hd:HD],
                                       c_rope[:, 1:2, 0:hd].broadcast_to([P, n, hd]), ALU.mult))
                c.link(v.tensor_tensor(rot_s[:, :, hd:HD], qk[:, :, 0:hd],
                                       c_rope[:, 1:2, hd:HD].broadcast_to([P, n, hd]), ALU.mult))
                v.tensor_tensor(q_rot[:, :, :], rot_c[:, 0:H1, :], rot_s[:, 0:H1, :], ALU.add)
                v.tensor_tensor(k_rep[:, :, :, :], rot_c[:, H1:n, :].unsqueeze(2).broadcast_to([P, KV1, REP, HD]),
                                rot_s[:, H1:n, :].unsqueeze(2).broadcast_to([P, KV1, REP, HD]), ALU.add).then_inc(b_rot, 1)

            def b_key_blocks(m):
                dve.wait_ge(b_kpose, m + 1)
                v.tensor_tensor(kBD_lo[:, :, :], pb1[:, 0:P].unsqueeze(1).broadcast_to([P, 2 * REP, P]),
                                c_blocks[:, :].unsqueeze(2).broadcast_to([P, 2 * REP, P]), ALU.mult)
                v.tensor_tensor(kBD_hi[0:KB, :, :], pb1[0:KB, P:2 * P].unsqueeze(1).broadcast_to([KB, REP, P]),
                                c_blocks[0:KB, 0:REP].unsqueeze(2).broadcast_to([KB, REP, P]),
                                ALU.mult).then_inc(b_kBDr, 1)

            def b_shift_scores(m):
                c = ch["b"]
                dve.wait_ge(b_s, m + 1)
                for src, lo, n in ((pb0, 0, 2 * REP), (pb1, 2 * REP, REP)):
                    s = src[:, 0:n * T].rearrange("p (h s) -> p h s", h=n)
                    c.mark(v.tensor_reduce(max1[:, lo:lo + n], s, axis=AX.X, op=ALU.max))
                c.wait()
                for src, lo, n in ((pb0, 0, 2 * REP), (pb1, 2 * REP, REP)):
                    s = src[:, 0:n * T].rearrange("p (h s) -> p h s", h=n)
                    last = v.tensor_tensor(s1[:, lo:lo + n, :], s, max1[:, lo:lo + n].unsqueeze(2).broadcast_to([P, n, T]),
                                           ALU.subtract)
                last.then_inc(b_shift, 1)

            def b_sums(m):
                c = ch["b"]
                dve.wait_ge(b_exp, m + 1)
                c.link(v.tensor_reduce(sum1[:, :], p1[:, :, 0:T], axis=AX.X, op=ALU.add))
                c.link(v.reciprocal(inv1[:, :], sum1[:, :]))

            def b_normalise(m):
                dve.wait_ge(b_o, m + 1)
                v.tensor_tensor(o1[:, :, :], pb0[:, 0:D].rearrange("p (h d) -> p h d", h=H1),
                                inv1[:, :].unsqueeze(2).broadcast_to([P, H1, HD]), ALU.mult).then_inc(b_or, 1)

            def b_residual(m):
                c = ch["b"]
                dve.wait_ge(b_y, m + 1)
                v.tensor_tensor(res_m[:, :], res_b[:, :], pb0[:, 0:D], ALU.add).then_inc(b_yread, 1)
                dve.wait_ge(b_yread, m + 1)
                moments(c, "b", res_m[:, :])
                v.tensor_copy(row(m), res_m[:, :])

            def b_finish(m):
                after_previous(dve, r_scattered, 16 * m)
                normalise(m, "b", moe_now[:, :], res_m[:, :]).then_inc(b_out, 1)

            def r_choose(m):
                c = ch["r"]
                c.tile(m)
                dve.wait_ge(r_l, m + 1)
                if not isinstance(m, int) or m < TILES - 1:
                    dve.wait_ge(b_vr, m + 2)
                c.link(v.tensor_tensor(lg[:, :], pb0[:, LG:LG + NE], c_rb[:, :], ALU.add))
                v.tensor_reduce(neg_max[:, :], lg[:, :], axis=AX.X, op=ALU.max, negate=True).then_inc(r_max, 1)
                dve.wait_ge(r_max, m + 1)
                c.link(v.tensor_scalar(best[:, :], lg[:, :], neg_max[:, :], 0.0, ALU.add, ALU.is_ge))
                c.link(v.tensor_tensor(best[:, :], best[:, :], c_prefer[:, :], ALU.mult))
                c.link(v.tensor_reduce(best_one[:, :], best[:, :], axis=AX.X, op=ALU.max))
                v.tensor_scalar(chosen[:, 0:NE], best[:, :], best_one[:, :], c_real[:, 0:1], ALU.is_equal,
                                ALU.mult).then_inc(r_onehot, 1)

            def r_slots(m):
                c = ch["r"]
                dve.wait_ge(r_ranked, m + 1)
                c.link(v.tensor_tensor(place[:, :], filled[:, :], pb0[:, RK:RK + NE + 1], ALU.add))
                c.link(v.tensor_tensor(filled[:, :], filled[:, :], pb0[:, TT:TT + NE + 1], ALU.add))
                v.scalar_tensor_tensor(place_one[:, :], place[:, :], 1.0, chosen[:, :], ALU.mult, ALU.mult,
                                       accum_out=slot_f[:, :]).then_inc(r_read, 1)
                dve.wait_ge(r_read, m + 1)
                dve.wait_ge(r_sum, m + 1)
                v.tensor_copy(slot_now[:, :], slot_f[:, :]).then_inc(r_slot, 1)
                if isinstance(m, int):
                    v.tensor_copy(slots[:, m:m + 1], slot_f[:, :])
                    v.reciprocal(max_prob[:, m:m + 1], exp_sum[:, :])
                else:
                    v.tensor_copy(slots[:, bass.ds(m, 1)], slot_f[:, :])
                    v.reciprocal(max_prob[:, bass.ds(m, 1)], exp_sum[:, :])

            overlapped(dve, (
                ("f", f_mean_x), ("t", t_convolve), ("f", f_quantise_x),
                ("r", r_choose), ("b", b_rotate), ("b", b_key_blocks), ("r", r_slots), ("t", t_pool),
                ("b", b_shift_scores), ("a", a_shift_scores), ("b", b_sums), ("f", f_silu),
                ("a", a_normalise), ("f", f_mean_y), ("b", b_normalise), ("f", f_quantise_y),
                ("t", t_moments), ("b", b_residual), ("f", f_residual), ("b", b_finish), ("a", a_residual),
                ("f", f_finish), ("t", t_norm), ("a", a_finish), ("t", t_finish)))
            n_plan = [n_setup[0]]

            def plan_step(ins):
                n_plan[0] += 1
                ins.then_inc(setup_dve, 1)
                dve.wait_ge(setup_dve, n_plan[0])
            dve.wait_ge(r_scattered, 16 * TILES)
            plan_step(v.tensor_tensor(tiles_of[:, :], filled[:, 0:NE], c_region[:, 0:NE], ALU.subtract))
            plan_step(v.tensor_scalar(tiles_of[:, :], tiles_of[:, :], 1.0 / P, (P - 1) / P - 0.5 + 0.5 / P, ALU.mult, ALU.add))
            plan_step(v.tensor_scalar(tiles_of[:, :], tiles_of[:, :], MAGIC, None, ALU.add))
            plan_step(v.tensor_scalar(tiles_of[:, :], tiles_of[:, :], MAGIC, None, ALU.subtract))
            plan_step(v.memset(tiles_before[:, 0:1], 0.0))
            for e in range(NE):
                plan_step(v.tensor_tensor(tiles_before[:, e + 1:e + 2], tiles_before[:, e:e + 1], tiles_of[:, e:e + 1], ALU.add))
            plan_step(v.tensor_scalar(jump[:, :], tiles_of[:, :], -float(P), float(CAP), ALU.mult, ALU.add))
            plan_step(v.memset(plan_f[:, EXPERT:EXPERT + MAX_TILES], 0.0))
            plan_step(v.tensor_scalar(plan_f[:, FIRST_ROW:FIRST_ROW + MAX_TILES], c_steps[:, :], float(P), None, ALU.mult))
            for e in range(1, NE):
                plan_step(v.tensor_scalar(reached[:, :], c_steps[:, :], tiles_before[:, e:e + 1], None, ALU.is_ge))
                at = plan_f[:, EXPERT:EXPERT + MAX_TILES]
                plan_step(v.tensor_tensor(at, at, reached[:, :], ALU.add))
                at = plan_f[:, FIRST_ROW:FIRST_ROW + MAX_TILES]
                plan_step(v.scalar_tensor_tensor(at, reached[:, :], jump[:, e - 1:e], at, ALU.mult, ALU.add))
            plan_step(v.tensor_copy(plan_f[:, PAD_ROW:PAD_ROW + NE], filled[:, 0:NE]))
            for k in range(3):
                plan_step(v.tensor_scalar(plan_f[:, STEPS + k:STEPS + k + 1], tiles_before[:, NE:NE + 1], float(k), None, ALU.subtract))
            plan_step(v.memset(e_xT[:, 1, :], 0.0))
            v.tensor_copy(plan[:, :], plan_f[:, :]).then_inc(planned, 1)
            e_chain = Chain(dve, chains["dve_m"])

            def e_silu(j):
                c = e_chain
                c.tile(j)
                dve.wait_ge(e_tanhr, j + 1)
                c.link(v.scalar_tensor_tensor(e_gate[:, :], e_tanh[:, :], 1.0, pa0[:, :], ALU.add, ALU.mult))
                dve.wait_ge(e_u, j + 1)
                after_previous(dve, e_ypose, j)
                v.scalar_tensor_tensor(e_y[:, :], e_gate[:, :], 0.5, pa1[:, :], ALU.mult, ALU.mult).then_inc(e_yr, 1)

            def e_round(j):
                dve.wait_ge(e_o, j + 1)
                after_previous(dve, e_stored, 16 * j)
                v.tensor_copy(e_out[:, :], pb1[:, 0:D]).then_inc(e_or, 1)
            for e in range(1, NE + 1):
                plan_step(v.tensor_scalar(slot_past[:, :], slots[:, :], float(e * CAP), jump[:, e - 1:e], ALU.is_ge, ALU.mult))
                plan_step(v.tensor_tensor(answer_at_f[:, :], slots[:, :] if e == 1 else answer_at_f[:, :], slot_past[:, :],
                                          ALU.subtract))
            v.tensor_copy(answer_at[:, :], answer_at_f[:, :]).then_inc(located, 1)
            total_steps = staggered(dve, (("g", e_silu), ("y", e_round)))
            dve.wait_ge(e_stored, 16 * total_steps)
            v.memset(e_spare[:, :], 0.0).then_inc(all_stored, 1)
            for g in range(GROUPS):
                ts = slice(g * GT, (g + 1) * GT)
                said = weighted[:, :, :]
                if g:
                    dve.wait_ge(finished, g)
                dve.wait_ge(gathered[g], 16 * GT)
                v.tensor_tensor(said, experts_said[:, ts, :], max_prob[:, ts].unsqueeze(2).broadcast_to([P, GT, D]),
                                ALU.mult).then_inc(scaled, 1)
                dve.wait_ge(scaled, g + 1)
                v.tensor_tensor(resid[:, ts, :], resid[:, ts, :], said, ALU.add).then_inc(finished, 1)


def _tables():
    import numpy as np
    c = {}
    ang = 2 * np.pi * np.outer(np.arange(D), np.arange(D)) / D
    full = np.concatenate([np.cos(ang), np.sin(ang)], 1)
    dft = np.zeros((P, KT, 2 * D), np.float32)
    dft[:, 0], dft[:KB, 1] = full[:P], full[P:]
    c["dft"] = dft
    ang = 2 * np.pi * np.outer(np.arange(T), np.arange(T)) / T
    seq = np.zeros((P, 2, P), np.float32)
    for b in range(2):
        s = slice(b * TP, b * TP + T)
        seq[s, 0, s], seq[s, 1, s] = np.cos(ang), -np.sin(ang)
    c["dft_seq"] = seq
    nb = NF // 2
    width = np.exp(np.log(T + 1) / nb).astype(np.float32) ** np.arange(1, nb + 1, dtype=np.float32) - np.float32(1)
    pos = np.arange(-T + 1, T, dtype=np.float32)
    near = (width[None, :] > np.abs(pos)[:, None]).astype(np.float32)
    c["rk_feat"] = np.ascontiguousarray(np.concatenate([near, np.sign(pos)[:, None] * near], 1).T)
    inv_freq = (1.0 / 10000.0 ** (np.arange(0, HD, 2, dtype=np.float32) / HD)).astype(np.float32)
    f = np.outer(np.arange(T, dtype=np.float32), inv_freq).astype(np.float32)
    rope = np.zeros((P, 2, HD), np.float32)
    for b in range(2):
        s = slice(b * TP, b * TP + T)
        rope[s, 0], rope[s, 1] = np.tile(np.cos(f), (1, 2)), np.concatenate([-np.sin(f), np.sin(f)], 1)
    c["rope"] = rope
    c["blocks"] = (np.arange(P)[:, None] // HD == np.arange(2 * REP)[None, :]).astype(np.float32)
    c["ident"] = np.eye(P, dtype=np.float32)
    c["tri"] = np.triu(np.ones((P, P), np.float32), 1)
    lanes = np.arange(P) % TP < T
    real = np.zeros((P, 2), np.float32)
    real[:, 0], real[:, 1] = lanes, ~lanes
    c["real"] = real
    c["prefer"] = np.ascontiguousarray(np.broadcast_to(np.arange(NE, 0, -1, dtype=np.float32), (P, NE)))
    c["region"] = np.ascontiguousarray(np.broadcast_to(np.arange(NE + 1, dtype=np.float32) * CAP, (P, NE + 1)))
    c["steps"] = np.ascontiguousarray(np.broadcast_to(np.arange(MAX_TILES, dtype=np.float32), (P, MAX_TILES)))
    return c


def _rows(w):
    import numpy as np
    out = np.zeros((P, KT) + w.shape[1:], np.float32)
    out[:, 0], out[:KB, 1] = w[:P], w[P:]
    return out


def kernel(**inputs):
    import numpy as np
    import concourse.bacc as bacc
    from concourse import mybir as mb
    from concourse.bass_utils import run_bass_kernel_spmd as run

    i = {k: np.asarray(v) for k, v in inputs.items()}
    c = _tables()
    wb = np.concatenate([i["L0_tok_w_dw"][:, 0, :], i["L0_tok_b_dw"][:, None]], 1)
    taps = np.stack([wb[:P], np.concatenate([wb[P:], wb[P:]])], 1)
    b_pw = np.zeros((P, KT), np.float32)
    b_pw[:, 0], b_pw[:KB, 1] = i["L0_tok_b_pw"][:P], i["L0_tok_b_pw"][P:]
    wp = i["L0_tok_w_pw"][:, :, 0].T
    w_pw = np.zeros((P, 3, D), np.float32)
    w_pw[:, 0], w_pw[:KB, 1], w_pw[KB:, 2] = wp[:P], wp[P:], wp[P:]
    wo0 = np.zeros((DV + 1, H0, D), np.float32)
    wo0[:DV] = i["L0_attn_Wo"].reshape(H0, DV, D).transpose(1, 0, 2)
    wo0[DV, 0] = i["L0_attn_bo"]
    bias_q = np.stack([i["L0_attn_r_w_bias"].reshape(HP, P).T, i["L0_attn_r_r_bias"].reshape(HP, P).T], 1)
    given = [
        ("x", i["x"]), ("taps", taps), ("w_pw", w_pw), ("b_pw", b_pw), ("dft", c["dft"]), ("dft_seq", c["dft_seq"]),
        ("gamma", i["L0_tok_gamma"]), ("beta", i["L0_tok_beta"]),
        ("wq0", _rows(i["L0_attn_Wq"])), ("wk0", _rows(i["L0_attn_Wk"])), ("wv0", _rows(i["L0_attn_Wv"])),
        ("wo0", wo0), ("rk_feat", c["rk_feat"]), ("wrk", i["L0_attn_Wrk"]), ("bias_q", bias_q),
        ("w_in", _rows(i["L0_ffn_w_in"].T)), ("g_in", i["L0_ffn_g_in"]),
        ("w_out", i["L0_ffn_w_out"].T.reshape(HID0 // P, P, D).transpose(1, 0, 2)), ("g_out", i["L0_ffn_g_out"]),
        ("wqkv1", _rows(np.concatenate([i["L1_attn_Wq"], i["L1_attn_Wk"], i["L1_attn_Wv"]]).T)),
        ("wo1", _rows(i["L1_attn_Wo"].T)), ("rope", c["rope"]), ("blocks", c["blocks"]), ("ident_in", c["ident"]),
        ("router_w", _rows(i["L1_ffn_router_w"])), ("router_b", i["L1_ffn_router_b"]),
        ("w1", i["L1_ffn_w1"]), ("w2", i["L1_ffn_w2"]), ("w3", i["L1_ffn_w3"]),
        ("tri", c["tri"]), ("real", c["real"]), ("prefer", c["prefer"]), ("region", c["region"]), ("steps", c["steps"]),
    ]
    nc = bacc.Bacc("TRN2", target_bir_lowering=False, num_devices=1)
    arrays, args = {}, {}
    for name, a in given:
        a = np.ascontiguousarray(a)
        arrays[f"in_{name}"] = a
        args[name] = nc.dram_tensor(f"in_{name}", a.shape, mb.dt.from_np(a.dtype), kind="ExternalInput").ap()
    args["out"] = nc.dram_tensor("out_0", (NB, T, D), mb.dt.float32, kind="ExternalOutput").ap()
    audio_tower(nc, **args)
    r = run(nc, [arrays], core_ids=[0])
    return r.results[0]["out_0"]
```

```python
import concourse.bass as bass
from concourse import mybir
from contextlib import ExitStack
import numpy as np

FP32 = mybir.dt.float32
BF16 = mybir.dt.bfloat16
I32 = mybir.dt.int32
ALU = mybir.AluOpType
ACT = mybir.ActivationFunctionType
AX = mybir.AxisListType

NB, SEQ, D = 64, 125, 192
TAPS = 7
T = SEQ // 2
TP = 64
P = 128
TILES = NB // 2
R_BEHIND = 3
E_PEELED = 3
HALO = TAPS // 2
XW = SEQ + 2 * HALO
PAIRS = 2 * T
H0, DK, DV, NF = 8, 64, 96, 32
HP = H0 // 2
REL = 2 * T - 1
RW = HP * REL
HID0 = 512
H1, KV1, HD = 12, 3, 16
REP = H1 // KV1
QKV1 = (H1 + 2 * KV1) * HD
NE, HID1 = 8, 512
KT = 2
KB = D - P
CAP = 4096
MAX_TILES = TILES + NE
MAGIC = 1.5 * 2.0 ** 23
EPS = 1e-5
EPS_RMS = 1e-6
SCALE1 = (HD * REP / H1) ** -0.5


def first(m):
    return isinstance(m, int) and m == 0


def after_previous(eng, sem, count):
    if not (isinstance(count, int) and count <= 0):
        eng.wait_ge(sem, count)


class Chain:

    def __init__(self, eng, sem):
        self.eng, self.sem, self.n, self.starts, self.per_tile, self.base = eng, sem, 0, {}, None, 0

    def stage(self, name, m):
        if first(m):
            self.starts[name] = self.n
            return
        if self.per_tile is None:
            self.per_tile = self.n
        self.base, self.n = m * self.per_tile + self.starts[name], 0

    def mark(self, ins):
        ins.then_inc(self.sem, 1)
        self.n += 1

    def wait(self, back=0):
        self.eng.wait_ge(self.sem, self.base + self.n - back)

    def link(self, ins):
        self.mark(ins)
        self.wait()


def audio_tower(nc, x, taps, w_pw, b_pw, dft, dft_seq, gamma, beta,
                wq0, wk0, wv0, wo0, rk_feat, wrk, bias_q, w_in, g_in, w_out, g_out,
                wqkv1, wo1, rope, blocks, ident_in, router_w, router_b, w1, w2, w3, tri, real, prefer, region, steps, out):
    LG, RK, TT = 2 * P + 32, 2 * P, 2 * P + 16
    routed = nc.dram_tensor("routed", ((NE + 1) * CAP, D), FP32).ap()
    answered = nc.dram_tensor("answered", (MAX_TILES * P, D), BF16).ap()
    rel_dram = nc.dram_tensor("rel_scores", (2 * TP, 2 * RW), FP32).ap()
    ctx = ExitStack()
    loop_mem = ExitStack()
    with ctx:
        def sb(name, shape, dt=FP32, mem=None):
            return (mem or ctx).enter_context(nc.sbuf_tensor(name, shape, dt))

        def sem(name):
            return ctx.enter_context(nc.semaphore(name))

        ident = sb("ident", [P, P])
        resid = sb("resid", [P, TILES, D])
        slots = sb("slots", [P, TILES])
        max_prob = sb("max_prob", [P, TILES])
        filled = sb("filled", [P, NE + 1])
        c_region = sb("c_region", [P, NE + 1])
        c_steps = sb("c_steps", [P, MAX_TILES])
        zeros = sb("zeros", [P, D])
        zeros16 = sb("zeros16", [P, D], BF16)
        w3_sb = sb("w3_sb", [P, NE, HID1 // P, D])
        pool_spare = sb("pool_spare", [P, 6])
        half = sb("half", [P, 1])
        c_eps = sb("c_eps", [P, 4])

        def lp(name, shape, dt=FP32):
            return sb(name, shape, dt, loop_mem)

        c_taps = lp("c_taps", [P, 2, TAPS + 1])
        c_bpw = lp("c_bpw", [P, 2])
        c_wpw = lp("c_wpw", [P, 3, D])
        c_dft = lp("c_dft", [P, KT, 2 * D])
        c_dft_seq = lp("c_dft_seq", [P, 2, P])
        c_gamma = lp("c_gamma", [P, D])
        c_beta = lp("c_beta", [P, D])
        x_tok = lp("x_tok", [SEQ, 2, D])
        xT_lo = lp("xT_lo", [P, 2, XW])
        xT_hi = lp("xT_hi", [P, XW])
        conv_lo = lp("conv_lo", [P, 2, PAIRS])
        conv_hi = lp("conv_hi", [P, PAIRS])
        pooled = lp("pooled", [P, KT, 2, T])
        hT = lp("hT", [P, KT, 2, TP])
        z_sb = lp("z_sb", [P, 2 * D])
        c_wq0 = lp("c_wq0", [P, KT, H0 * DK])
        c_wk0 = lp("c_wk0", [P, KT, H0 * DK])
        c_wv0 = lp("c_wv0", [P, KT, H0 * DV])
        c_wo0 = lp("c_wo0", [DV + 1, H0, D])
        c_feat = lp("c_feat", [NF, REL])
        c_wrk = lp("c_wrk", [NF, H0 * DK])
        c_bias_q = lp("c_bias_q", [P, 2, HP])
        rkBD = lp("rkBD", [P, HP, 2, REL])
        a_in = lp("a_in", [P, D])
        res_a, res_f, res_b, res_m = (lp(f"res_{k}", [P, D]) for k in "afbm")
        hold_a = lp("hold_a", [P, D])
        a_xT = lp("a_xT", [P, KT, P])
        q8 = lp("q8", [P, HP, P])
        qr = lp("qr", [P, HP, P])
        qBD = lp("qBD", [P, HP, 2, 2, TP])
        kT0 = lp("kT0", [P, HP, P])
        v0 = lp("v0", [P, H0 * DV])
        rel_tok = lp("rel_tok", [P, 2, REL, HP])
        rel_skew = lp("rel_skew", [P, 2, T, HP])
        s0 = lp("s0", [P, H0, T])
        p0 = lp("p0", [P, HP, 2, TP])
        pT0 = lp("pT0", [P, H0, 2, TP])
        oT0 = lp("oT0", [DV + 1, H0, P])
        c_win_f = lp("c_win_f", [P, KT, 2 * HID0])
        c_wout_f = lp("c_wout_f", [P, HID0 // P, D])
        c_win = lp("c_win", [P, KT, 2 * HID0], BF16)
        c_wout = lp("c_wout", [P, HID0 // P, D], BF16)
        c_gin = lp("c_gin", [P, D])
        c_gout = lp("c_gout", [P, HID0])
        ident16 = lp("ident16", [P, P], BF16)
        wsum = lp("wsum", [P, 2])
        wsc = lp("wsc", [P, 4])
        f_in = lp("f_in", [P, D])
        f_sq = lp("f_sq", [P, HID0])
        f_x = lp("f_x", [P, D])
        f_xq = lp("f_xq", [P, D], BF16)
        f_xqT = lp("f_xqT", [P, KT, P], BF16)
        f_tanh = lp("f_tanh", [P, HID0])
        f_gate = lp("f_gate", [P, HID0])
        f_y = lp("f_y", [P, HID0])
        f_yq = lp("f_yq", [P, HID0], BF16)
        f_yqT = lp("f_yqT", [P, HID0 // P, P], BF16)
        c_wqkv1 = lp("c_wqkv1", [P, KT, QKV1])
        c_wo1 = lp("c_wo1", [P, KT, D])
        c_rope = lp("c_rope", [P, 2, HD])
        c_blocks = lp("c_blocks", [P, 2 * REP])
        b_in = lp("b_in", [P, D])
        b_xT = lp("b_xT", [P, KT, P])
        rot_c = lp("rot_c", [P, H1 + KV1, HD])
        rot_s = lp("rot_s", [P, H1 + KV1, HD])
        q_rot = lp("q_rot", [P, H1, HD])
        k_rep = lp("k_rep", [P, KV1, REP, HD])
        vBD = lp("vBD", [P, 2, KV1, 2, HD + 1])
        qT1 = lp("qT1", [P, KT, P])
        kBD_lo = lp("kBD_lo", [P, 2 * REP, P])
        kBD_hi = lp("kBD_hi", [P, REP, P])
        p1 = lp("p1", [P, H1, TP])
        pT1 = lp("pT1", [P, H1 // 2, P])
        o1 = lp("o1", [P, H1, HD])
        oT1 = lp("oT1", [P, KT, P])
        moe_now = lp("moe_now", [P, D])
        r_xT = lp("r_xT", [P, KT, P])
        lg, r_exp, best = lp("lg", [P, NE]), lp("r_exp", [P, NE]), lp("best", [P, NE])
        neg_max, exp_sum, best_one, slot_f = (lp(k, [P, 1]) for k in ("neg_max", "exp_sum", "best_one", "slot_f"))
        slot_now = lp("slot_now", [P, 1], I32)
        chosen = lp("chosen", [P, NE + 1])
        place, place_one = lp("place", [P, NE + 1]), lp("place_one", [P, NE + 1])
        c_tri = lp("c_tri", [P, P])
        c_prefer = lp("c_prefer", [P, NE])
        c_real = lp("c_real", [P, 2])
        c_rw = lp("c_rw", [P, KT, NE])
        c_rb = lp("c_rb", [P, NE])
        spare = lp("spare", [1, 1])
        ones = lp("ones", [P, P])
        st = {k: lp(f"stats_{k}", [P, 6]) for k in ("t1", "t2", "a", "f", "b")}
        mv = {k: lp(f"meanvar_{k}", [P, 2]) for k in ("t1", "t2", "a", "f", "b")}
        var = {k: lp(f"var_{k}", [P, 1]) for k in ("t1", "t2", "a", "f", "b", "x", "y")}
        rstd = {k: lp(f"rstd_{k}", [P, 1]) for k in ("t1", "t2", "a", "f", "b", "x", "y")}
        ssq = {k: lp(f"ssq_{k}", [P, 1]) for k in ("x", "y")}
        amax = {k: lp(f"amax_{k}", [P, 1]) for k in ("x", "y")}
        qsc = {k: lp(f"qscale_{k}", [P, 2]) for k in ("x", "y")}
        unit = {k: lp(f"quant_unit_{k}", [P, 1]) for k in ("x", "y")}
        dq = {k: lp(f"dequant_{k}", [P, 3]) for k in ("x", "y")}
        max0 = lp("max0", [P, H0])
        sum0 = lp("sum0", [P, H0])
        inv0 = lp("inv0", [P, H0])
        max1 = lp("max1", [P, H1])
        inv1 = lp("inv1", [P, H1])

        def bank(name):
            return ctx.enter_context(nc.psum_tensor(name, [P, 512], FP32))
        pt, pa0, pa1, pa2, pf0, pf1, pb0, pb1 = (bank(f"bank_{k}") for k in (
            "t", "a0", "a1", "a2", "f0", "f1", "b0", "b1"))

        w_t, w_a, w_f, w_b = sem("weights_t"), sem("weights_a"), sem("weights_f"), sem("weights_b")
        cleared, cleared_dve, half_set = sem("cleared"), sem("cleared_dve"), sem("half_set")
        rk_done, rk_stored = sem("rk_done"), sem("rk_stored")
        wabs, wtotal, wtern = sem("wabs"), sem("wtotal"), sem("wtern")
        setup_dve, w_e, answers_cleared = sem("setup_dve"), sem("weights_e"), sem("answers_cleared")
        x_loaded, t_xpose, t_xT, t_conv, t_pw, t_pooled, t_h, t_z, t_zs, t_y = (sem(f"t_{k}") for k in (
            "x_loaded", "transposed", "xT_ready", "conv_done", "pointwise_done", "pooled", "h_ready",
            "z_done", "z_ready", "y_done"))
        t_yread, t_out = sem("t_y_read"), sem("t_out_ready")
        var_eps = {k: sem(f"var_eps_added_{k}") for k in var}
        pads_chosen, r_kept = sem("padding_rows_chosen"), sem("r_slots_kept")
        f_yread, a_q8r = sem("f_y_read"), sem("a_q_ready")
        a_kept, b_kept, t_mtap = sem("a_residual_kept"), sem("b_residual_kept"), sem("t_middle_tap_ready")
        var_ready = {k: sem(f"var_ready_{k}") for k in var}
        rstd_ready = {k: sem(f"rstd_ready_{k}") for k in var}
        (a_xpose, a_xTr, a_q, a_k, a_v1, a_v2, a_qrr, a_qbd, a_kr, a_v1r, a_v2r, a_r, a_rs, a_wr, a_rel, a_s,
         a_shift, a_exp, a_p, a_pt, a_ptr, a_o, a_or, a_y, a_yread, a_out) = (sem(f"a_{k}") for k in (
            "transposed", "xT_ready", "q_done", "k_done", "v_lo_done", "v_hi_done", "qr_ready", "q_blocks_ready",
            "k_ready", "v_lo_ready", "v_hi_ready", "rel_done", "rel_ready", "rel_written", "rel_skewed",
            "scores_done", "shifted", "exp_ready", "probs_ready", "probs_transposed", "pT_ready", "heads_done",
            "heads_ready", "y_done", "y_read", "out_ready"))
        (f_xqr, f_xpose, f_xTr, f_up, f_gt, f_tanhr, f_yr, f_yqr, f_ypose, f_yTr, f_o, f_out) = (
            sem(f"f_{k}") for k in ("x_quantised", "x_transposed", "xT_ready", "up_done", "gate_done",
                                    "tanh_ready", "y_ready", "y_quantised", "y_transposed",
                                    "yT_ready", "down_done", "out_ready"))
        (b_xpose, b_xTr, b_qkv, b_vr, b_rot, b_qpose, b_kpose, b_qTr, b_kBDr, b_s, b_shift, b_exp, b_pt, b_ptr,
         b_o, b_or, b_opose, b_oTr, b_y, b_yread, b_out) = (sem(f"b_{k}") for k in (
            "transposed", "xT_ready", "qkv_done", "v_ready", "rotated", "q_transposed", "k_transposed", "qT_ready",
            "k_blocks_ready", "scores_done", "shifted", "exp_ready", "probs_transposed", "pT_ready",
            "heads_done", "heads_ready", "heads_transposed", "oT_ready", "y_done", "y_read", "out_ready"))
        (r_xpose, r_xTr, r_l, r_max, r_sum, r_onehot, r_ranked, r_read, r_slot, r_scattered) = (sem(f"r_{k}") for k in (
            "transposed", "xT_ready", "logits_done", "max_ready", "exp_sum_ready", "chosen", "ranks_done", "ranks_read",
            "slots_ready", "scattered"))
        chains = {k: sem(f"chain_{k}") for k in ("dve_t", "dve_a", "dve_f", "dve_b", "dve_r", "dve_m")}

        loop_mem.close()
        w1_sb = sb("w1_sb", [P, NE, KT, HID1])
        w2_sb = sb("w2_sb", [P, NE, KT, HID1])
        e_tok = sb("e_tok", [P, D])
        e_xT = sb("e_xT", [P, KT, P])
        e_tanh = sb("e_tanh", [P, HID1])
        e_gate = sb("e_gate", [P, HID1])
        e_y = sb("e_y", [P, HID1])
        e_yT = sb("e_yT", [P, HID1 // P, P])
        e_out = sb("e_out", [P, D], BF16)
        experts_said = sb("experts_said", [P, TILES, D], BF16)
        EXPERT, FIRST_ROW, PAD_ROW, STEPS = 0, MAX_TILES, 2 * MAX_TILES, 2 * MAX_TILES + NE
        plan = sb("plan", [P, STEPS + 3], I32)
        plan_f = sb("plan_f", [P, STEPS + 3])
        tiles_of = sb("tiles_of", [P, NE])
        tiles_before = sb("tiles_before", [P, NE + 1])
        jump = sb("jump", [P, NE])
        reached = sb("reached", [P, MAX_TILES])
        slot_past = sb("slot_past", [P, TILES])
        answer_at_f = sb("answer_at_f", [P, TILES])
        answer_at = sb("answer_at", [P, TILES], I32)
        e_spare = sb("e_spare", [1, 1])
        weighted = sb("weighted", [P, TILES // 4, D])
        planned, pads_written, located = sem("planned"), sem("pads_written"), sem("answers_located")
        (e_loaded, e_xpose, e_xTr, e_g, e_u, e_tanhr, e_yr, e_ypose, e_yTr, e_o, e_or, e_stored, all_stored) = (sem(f"e_{k}") for k in (
            "x_loaded", "transposed", "xT_ready", "gate_done", "up_done", "tanh_ready", "y_ready", "y_transposed",
            "yT_ready", "down_done", "out_ready", "stored", "all_stored"))
        WEIGHT_GROUPS, GE = 4, NE // 4
        w_group = sem("weights_group")
        w_ready = sem("expert_weights_ready")
        w_spare = sb("w_spare", [P, NE])
        scaled, finished, stored = (sem(k) for k in ("scaled", "finished", "stored"))
        GROUPS, GT = 4, TILES // 4
        gathered = [sem(f"gathered_{g}") for g in range(GROUPS)]

        def staggered(eng, stages):
            lag = {"x": 0, "g": 1, "y": 2}
            eng.wait_ge(planned, 1)
            total, last, last_but_one = (
                eng.value_load(plan[0:1, STEPS + k:STEPS + k + 1], min_val=TILES - 1 - k, max_val=MAX_TILES - k) for k in range(3))

            def body(steps):
                for name, stage in stages:
                    if name in steps:
                        stage(steps[name])
            for j in range(E_PEELED):
                body({name: j - late for name, late in lag.items() if j >= late})
            with eng.Fori(E_PEELED, total) as j:
                body({name: j - late for name, late in lag.items()})
            body({"g": last, "y": last_but_one})
            body({"y": last})
            return total

        block = ctx.enter_context(nc.Block())
        LOADS_T, LOADS_A, LOADS_F, LOADS_B = 9 * 16, 7 * 16, 5 * 16, 10 * 16

        def overlapped(eng, stages):
            def body(n):
                for late, stage in stages:
                    m = n - late
                    if not isinstance(m, int) or 0 <= m < TILES:
                        stage(m)
            peeled = max(late for late, stage in stages)
            for n in range(peeled + 1):
                body(n)
            with eng.Fori(peeled + 1, TILES) as n:
                body(n)
            for n in range(TILES, TILES + peeled):
                body(n)

        @block.sync
        def _(sp):
            def load_x(m):
                src = x[bass.ds(sp.snap(2 * m), 2)] if not isinstance(m, int) else x[2 * m:2 * m + 2]
                if not first(m):
                    sp.wait_ge(t_xpose, m)
                sp.dma_start(x_tok[:, :, :], src.rearrange("b s c -> s b c")).then_inc(x_loaded, 16)

            sp.dma_start(ident[:, :], ident_in).then_inc(w_t, 16)
            load_x(0)
            sp.dma_start(c_taps[:, :, :], taps).then_inc(w_t, 16)
            sp.dma_start(c_bpw[:, :], b_pw).then_inc(w_t, 16)
            sp.dma_start(c_wpw[:, :, :], w_pw).then_inc(w_t, 16)
            sp.dma_start(c_dft[:, :, :], dft).then_inc(w_t, 16)
            sp.dma_start(c_dft_seq[:, :, :], dft_seq).then_inc(w_t, 16)
            sp.dma_start(c_gamma[:, :], bass.AP(gamma.tensor, 0, [[0, P], [1, D]])).then_inc(w_t, 16)
            sp.dma_start(c_beta[:, :], bass.AP(beta.tensor, 0, [[0, P], [1, D]])).then_inc(w_t, 16)
            sp.dma_start(c_feat[:, :], rk_feat).then_inc(w_t, 16)
            sp.dma_start(c_wrk[:, :], wrk).then_inc(w_a, 16)
            sp.dma_start(c_bias_q[:, :, :], bias_q).then_inc(w_a, 16)
            sp.dma_start(c_wq0[:, :, :], wq0).then_inc(w_a, 16)
            sp.dma_start(c_wk0[:, :, :], wk0).then_inc(w_a, 16)
            sp.dma_start(c_wv0[:, :, :], wv0).then_inc(w_a, 16)
            sp.dma_start(c_wo0[:, :, :], wo0).then_inc(w_a, 16)
            sp.dma_start(c_rw[:, :, :], router_w).then_inc(w_a, 16)
            sp.dma_start(c_win_f[:, :, :], w_in).then_inc(w_f, 16)
            sp.dma_start(c_wout_f[:, :, :], w_out).then_inc(w_f, 16)
            sp.dma_start(c_gin[:, :], bass.AP(g_in.tensor, 0, [[0, P], [1, D]])).then_inc(w_f, 16)
            sp.dma_start(c_gout[:, :], bass.AP(g_out.tensor, 0, [[0, P], [1, HID0]])).then_inc(w_f, 16)
            sp.dma_start(c_rb[:, :], bass.AP(router_b.tensor, 0, [[0, P], [1, NE]])).then_inc(w_f, 16)
            sp.dma_start(c_wqkv1[:, :, :], wqkv1).then_inc(w_b, 16)
            sp.dma_start(c_wo1[:, :, :], wo1).then_inc(w_b, 16)
            sp.dma_start(c_rope[:, :, :], rope).then_inc(w_b, 16)
            sp.dma_start(c_blocks[:, :], blocks).then_inc(w_b, 16)
            sp.dma_start(w3_sb[:, :, :, :], w3.rearrange("e (k p) d -> p e k d", p=P)).then_inc(w_e, 16)
            sp.wait_ge(cleared, 5)
            sp.dma_start(answered.rearrange("(a p) d -> p a d", p=P),
                         zeros16[:, :].unsqueeze(1).broadcast_to([P, MAX_TILES, D])).then_inc(answers_cleared, 16)
            sp.dma_start(c_tri[:, :], tri).then_inc(w_b, 16)
            sp.dma_start(c_prefer[:, :], prefer).then_inc(w_b, 16)
            sp.dma_start(c_real[:, :], real).then_inc(w_b, 16)
            sp.dma_start(filled[:, :], region).then_inc(w_b, 16)
            sp.dma_start(c_region[:, :], region).then_inc(w_b, 16)
            sp.dma_start(c_steps[:, :], steps).then_inc(w_b, 16)

            def t_load_x(m):
                if not first(m):
                    load_x(m)

            def a_skew(m):
                written = 16 * m + 16 if isinstance(m, int) else sp.snap(16 * m + 16)
                used = m if isinstance(m, int) else sp.snap(m)
                after_previous(sp, a_rel, 32 * m)
                sp.wait_ge(a_rs, 2 * m + 2)
                sp.dma_start(rel_dram, rel_tok[:, :, :, :].rearrange("p a r h -> p (a r h)")).then_inc(a_wr, 16)
                sp.wait_ge(a_wr, written)
                if not first(m):
                    sp.wait_ge(a_shift, used)
                for h2 in range(2):
                    sp.dma_start(
                        rel_skew[TP * h2:TP * h2 + TP, :, :, :].rearrange("p b s h -> p b (s h)"),
                        bass.AP(rel_dram.tensor, h2 * RW + (T - 1) * HP,
                                [[2 * RW - HP, TP], [2 * RW * TP, 2], [1, T * HP]])).then_inc(a_rel, 16)

            overlapped(sp, (
                (2, a_skew), (0, t_load_x)))
            sp.wait_ge(r_scattered, 16 * TILES)
            sp.wait_ge(planned, 1)
            sp.wait_ge(answers_cleared, 16)
            for e in range(NE):
                at = sp.value_load(plan[0:1, PAD_ROW + e:PAD_ROW + e + 1], min_val=0, max_val=NE * CAP)
                sp.dma_start(routed[bass.ds(at, P), :], zeros[:, :]).then_inc(pads_written, 16)
            sp.wait_ge(pads_written, 16 * NE)

            def first_row(j):
                at = plan[0:1, FIRST_ROW + j:FIRST_ROW + j + 1] if isinstance(j, int) else plan[0:1, bass.ds(j + FIRST_ROW, 1)]
                return sp.value_load(at, min_val=0, max_val=NE * CAP)

            def load_rows(j):
                src = routed[bass.ds(first_row(j), P), :]
                if not first(j):
                    sp.wait_ge(e_xpose, j)
                sp.dma_start(e_tok[:, :], src).then_inc(e_loaded, 16)
            total_steps = staggered(sp, (("x", load_rows),))
            for g in range(GROUPS):
                sp.wait_ge(finished, g + 1)
                for b in range(2):
                    sp.dma_start(out.rearrange("(m two) t c -> two t m c", two=2)[b][:, g * GT:(g + 1) * GT, :],
                                 resid[b * TP:b * TP + T, g * GT:(g + 1) * GT, :]).then_inc(stored, 16)
            sp.wait_ge(stored, 16 * 2 * GROUPS)

        @block.gpsimd
        def _(pool):
            for dst, value in ((half[:, :], -0.5), (c_eps[:, 0:1], EPS), (c_eps[:, 1:2], EPS_RMS), (c_eps[:, 2:3], 1.0 / D),
                               (c_eps[:, 3:4], 1.0 / HID0)):
                pool.memset(dst, value).then_inc(half_set, 1)
            pool.wait_ge(half_set, 5)
            for t_ in (rkBD, qBD, p0, a_xT, pT0, f_xqT, vBD, qT1, kBD_hi, p1, oT1, b_xT, r_xT):
                a = t_[tuple(slice(None) for _ in t_.shape)]
                last = pool.memset(a, 0.0)
            last.then_inc(cleared, 1)
            pool.wait_ge(cleared, 1)
            pool.memset(oT0[DV:DV + 1, :, :], 1.0).then_inc(cleared, 1)
            pool.wait_ge(cleared, 2)
            pool.memset(ones[:, :], 1.0).then_inc(cleared, 1)
            pool.wait_ge(cleared, 3)
            pool.memset(zeros[:, :], 0.0).then_inc(cleared, 1)
            pool.wait_ge(cleared, 4)
            pool.memset(zeros16[:, :], 0.0).then_inc(cleared, 1)

            def inv_sqrt(k, width=None):
                def stage(m):
                    pool.wait_ge(var_ready[k], m + 1)
                    added = pool.tensor_tensor(out=var[k][:, :], in0=mv[k][:, 1:2], in1=c_eps[:, 0:1], op=ALU.add)
                    added.then_inc(var_eps[k], 1)
                    pool.wait_ge(var_eps[k], m + 1)
                    pool.tensor_tensor(out=rstd[k][:, :], in0=var[k][:, :], in1=half[:, :],
                                       op=ALU.pow).then_inc(rstd_ready[k], 1)

                def stage_rms(m):
                    pool.wait_ge(var_ready[k], m + 1)
                    pool.tensor_tensor(out=var[k][:, :], in0=ssq[k][:, :], in1=c_eps[:, width:width + 1],
                                       op=ALU.mult).then_inc(var_eps[k], 1)
                    pool.wait_ge(var_eps[k], 2 * m + 1)
                    pool.tensor_tensor(out=var[k][:, :], in0=var[k][:, :], in1=c_eps[:, 1:2],
                                       op=ALU.add).then_inc(var_eps[k], 1)
                    pool.wait_ge(var_eps[k], 2 * m + 2)
                    pool.tensor_tensor(out=rstd[k][:, :], in0=var[k][:, :], in1=half[:, :],
                                       op=ALU.pow).then_inc(rstd_ready[k], 1)
                return stage if width is None else stage_rms

            def spare_of(k):
                at = ("t2", "a", "f", "b", "keep", "scatter").index(k)
                return pool_spare[:, at:at + 1]

            def normalise(m, k, dst, src, done):
                pool.wait_ge(rstd_ready[k], m + 1)
                pool.tensor_tensor(out=spare_of(k), in0=half[:, :], in1=half[:, :], op=ALU.add)
                pool.tensor_scalar(dst[:, :], src[:, :], mv[k][:, 0:1], rstd[k][:, :], ALU.subtract, ALU.mult).then_inc(done, 1)

            def t_finish(m):
                inv_sqrt("t2")(m)
                after_previous(pool, a_xpose, m)
                normalise(m, "t2", a_in, res_a, t_out)

            def a_keep(m):
                after_previous(pool, a_yread, m)
                pool.tensor_tensor(out=spare_of("keep"), in0=half[:, :], in1=half[:, :], op=ALU.add)
                pool.tensor_copy(hold_a[:, :], res_a[:, :]).then_inc(a_kept, 1)

            def a_finish(m):
                inv_sqrt("a")(m)
                after_previous(pool, f_xqr, m)
                normalise(m, "a", f_in, res_f, a_out)

            def f_finish(m):
                inv_sqrt("f")(m)
                after_previous(pool, b_xpose, m)
                normalise(m, "f", b_in, res_b, f_out)

            def b_finish(m):
                inv_sqrt("b")(m)
                after_previous(pool, r_scattered, 16 * m)
                normalise(m, "b", moe_now, res_m, b_out)
            t_inv_sqrt, f_inv_sqrt_x, f_inv_sqrt_y = inv_sqrt("t1"), inv_sqrt("x", 2), inv_sqrt("y", 3)

            def r_scatter(m):
                pool.wait_ge(r_slot, m + 1)
                pool.tensor_tensor(out=spare_of("scatter"), in0=half[:, :], in1=half[:, :], op=ALU.add)
                pool.indirect_dma_start(out=routed, out_offset=bass.IndirectOffsetOnAxis(ap=slot_now[:, 0:1], axis=0),
                                        in_=moe_now[:, :], in_offset=None).then_inc(r_scattered, 16)
            overlapped(pool, (
                (3, f_inv_sqrt_x), (3, f_inv_sqrt_y), (1, t_inv_sqrt), (3, f_finish), (1, t_finish), (5, r_scatter),
                (1, a_keep), (2, a_finish), (4, b_finish)))
            pool.wait_ge(r_kept, TILES)
            pool.wait_ge(r_scattered, 16 * TILES)
            for g in range(WEIGHT_GROUPS):
                es = slice(g * GE, (g + 1) * GE)
                for w, src in ((w1_sb, w1), (w2_sb, w2)):
                    pool.dma_start(w[:, es, 0, :], src[es, 0:P, :].rearrange("e p n -> p e n")).then_inc(w_group, 16)
                    pool.dma_start(w[0:KB, es, 1, :], src[es, P:D, :].rearrange("e p n -> p e n")).then_inc(w_group, 16)
                pool.wait_ge(w_group, 64 * (g + 1))
                for e in range(GE):
                    pool.tensor_tensor(out=w_spare[:, g * GE + e:g * GE + e + 1], in0=half[:, :], in1=half[:, :],
                                       op=ALU.add).then_inc(w_ready, 1)
            pool.wait_ge(located, 1)
            pool.wait_ge(all_stored, 1)
            for m in range(TILES):
                pool.indirect_dma_start(out=experts_said[:, m, :], out_offset=None, in_=answered,
                                        in_offset=bass.IndirectOffsetOnAxis(ap=answer_at[:, m:m + 1], axis=0)).then_inc(gathered[m // GT], 16)

        @block.tensor
        def _(pe):
            def mm(dst, lhsT, rhs, start=True, stop=True):
                return nc.tensor.matmul(dst, lhsT, rhs, start=start, stop=stop)

            def xpose(dst, src, idn=None):
                return nc.tensor.transpose(dst, src, ident[0:src.shape[0], 0:src.shape[0]] if idn is None else idn)

            def xpose_rows(dst, src, sig):
                xpose(dst[:, 0:P], src[:, 0:P])
                xpose(dst[0:KB, P:2 * P], src[:, P:D]).then_inc(sig, 1)

            def prepare():
                pe.wait_ge(w_a, LOADS_A)
                for hp in range(HP):
                    last = mm(pa0[:, hp * REL:(hp + 1) * REL], c_wrk[:, hp * P:(hp + 1) * P], c_feat[:, :])
                last.then_inc(rk_done, 1)
                pe.wait_ge(wabs, 2)
                pe.wait_ge(cleared, 3)
                mm(pf0[:, 0:2], ones[:, :], wsum[:, :]).then_inc(wtotal, 1)
                pe.wait_ge(rk_stored, 1)

            def t_transpose(m):
                pe.wait_ge(x_loaded, 16 * m + 16)
                after_previous(pe, t_yread, m)
                for b in range(2):
                    xpose(pt[:, b * SEQ:(b + 1) * SEQ], x_tok[:, b, 0:P])
                for b in range(2):
                    last = xpose(pt[0:KB, (2 + b) * SEQ:(3 + b) * SEQ], x_tok[:, b, P:D])
                last.then_inc(t_xpose, 1)

            def t_pointwise(m):
                pe.wait_ge(t_conv, m + 1)
                for lo, hi, at in ((0, P, 0), (P, D, 2 * PAIRS)):
                    dst = pt[0:hi - lo, at:at + 2 * PAIRS]
                    mm(dst, c_wpw[:, 0, lo:hi], conv_lo[:, :, :].rearrange("p b s -> p (b s)"), stop=False)
                    mm(dst[:, 0:PAIRS], c_wpw[:, 1, lo:hi], conv_hi[:, :], start=False, stop=False)
                    last = mm(dst[:, PAIRS:2 * PAIRS], c_wpw[:, 2, lo:hi], conv_hi[:, :], start=False)
                last.then_inc(t_pw, 1)

            def t_dft(m):
                pe.wait_ge(t_h, m + 1)
                for kt in range(KT):
                    last = mm(pt[:, 0:2 * D], hT[:, kt, :, :].rearrange("p b s -> p (b s)"), c_dft[:, kt, :],
                              start=kt == 0, stop=kt == KT - 1)
                last.then_inc(t_z, 1)

            def t_dft_seq(m):
                pe.wait_ge(t_zs, m + 1)
                mm(pt[:, 0:D], c_dft_seq[:, 0, :], z_sb[:, 0:D], stop=False)
                mm(pt[:, 0:D], c_dft_seq[:, 1, :], z_sb[:, D:2 * D], start=False).then_inc(t_y, 1)

            def a_transpose(m):
                if first(m):
                    prepare()
                pe.wait_ge(t_out, m + 1)
                after_previous(pe, a_v2r, m)
                if not isinstance(m, int) or m > R_BEHIND:
                    pe.wait_ge(r_read, m - R_BEHIND)
                xpose_rows(pa0, a_in, a_xpose)

            def a_project_q(m):
                pe.wait_ge(a_xTr, m + 1)
                project(c_wq0, pa0, a_q)

            def a_project_k(m):
                pe.wait_ge(a_q8r, m + 1)
                project(c_wk0, pa0, a_k)

            def project(w, dst, sig):
                for hp in range(HP):
                    for kt in range(KT):
                        last = mm(dst[:, hp * P:(hp + 1) * P], w[:, kt, hp * P:(hp + 1) * P], a_xT[:, kt, :],
                                  start=kt == 0, stop=kt == KT - 1)
                last.then_inc(sig, 1)

            def a_relative(i):
                def stage(m):
                    if i == 0:
                        pe.wait_ge(a_kr, m + 1)
                        pe.wait_ge(a_qrr, m + 1)
                    else:
                        pe.wait_ge(a_rs, 2 * m + 1)
                    for k in range(2):
                        last = mm(pa0[:, k * 2 * REL:(k + 1) * 2 * REL], qr[:, 2 * i + k, :],
                                  rkBD[:, 2 * i + k, :, :].rearrange("p a r -> p (a r)"))
                    last.then_inc(a_r, 1)
                return stage
            a_relative_lo, a_relative_hi = a_relative(0), a_relative(1)

            def a_project_v(m):
                pe.wait_ge(a_rs, 2 * m + 2)
                for kt in range(KT):
                    last = mm(pa0[:, :], a_xT[:, kt, :], c_wv0[:, kt, 0:512], start=kt == 0, stop=kt == KT - 1)
                last.then_inc(a_v1, 1)

            def a_project_v_rest(m):
                pe.wait_ge(a_v1r, m + 1)
                for kt in range(KT):
                    last = mm(pa0[:, 0:H0 * DV - 512], a_xT[:, kt, :], c_wv0[:, kt, 512:H0 * DV],
                              start=kt == 0, stop=kt == KT - 1)
                last.then_inc(a_v2, 1)

            def a_scores(m):
                pe.wait_ge(a_kr, m + 1)
                pe.wait_ge(a_qbd, m + 1)
                after_previous(pe, a_yread, m)
                for hp in range(HP):
                    for b in range(2):
                        at = (hp * 2 + b) * T
                        last = mm(pa1[:, at:at + T], qBD[:, hp, b, :, :].rearrange("p a t -> p (a t)"), kT0[:, hp, b * TP:b * TP + T])
                last.then_inc(a_s, 1)

            def a_probs_transpose(m):
                pe.wait_ge(a_p, m + 1)
                for hp in range(HP):
                    last = xpose(pa2[:, hp * P:(hp + 1) * P], p0[:, hp, :, :].rearrange("p b s -> p (b s)"))
                last.then_inc(a_pt, 1)

            def a_values(m):
                pe.wait_ge(a_ptr, m + 1)
                pe.wait_ge(a_v2r, m + 1)
                for h in range(H0):
                    last = mm((pa1, pa2)[h // 4][0:DV, (h % 4) * P:(h % 4 + 1) * P], v0[:, h * DV:(h + 1) * DV],
                              pT0[:, h, :, :].rearrange("p b t -> p (b t)"))
                    if h % 4 == 3:
                        last.then_inc(a_o, 1)

            def a_output(m):
                pe.wait_ge(a_or, 2 * m + 2)
                for h in range(H0):
                    k = DV + 1 if h == 0 else DV
                    last = mm(pa1[:, 0:D], oT0[0:k, h, :], c_wo0[0:k, h, :], start=h == 0, stop=h == H0 - 1)
                last.then_inc(a_y, 1)

            def f_transpose_x(m):
                if first(m):
                    pe.wait_ge(wtern, 1)
                pe.wait_ge(f_xqr, m + 1)
                pe_free_f(m)
                d = pf0[:, :].bitcast(BF16)
                xpose(d[:, 0:P], f_xq[:, 0:P], ident16[:, :])
                xpose(d[0:KB, P:2 * P], f_xq[:, P:D], ident16[:, :]).then_inc(f_xpose, 1)

            def pe_free_f(m):
                after_previous(pe, f_yread, m)

            def f_up_gate(m):
                pe.wait_ge(f_xTr, m + 1)
                for dst, at, sig in ((pf0, 0, f_up), (pf1, HID0, f_gt)):
                    for kt in range(KT):
                        last = mm(dst[:, :], f_xqT[:, kt, :], c_win[:, kt, at:at + HID0], start=kt == 0, stop=kt == KT - 1)
                    last.then_inc(sig, 1)

            def f_transpose_y(m):
                pe.wait_ge(f_yqr, m + 1)
                d = pf0[:, :].bitcast(BF16)
                for j in range(HID0 // P):
                    last = xpose(d[:, j * P:(j + 1) * P], f_yq[:, j * P:(j + 1) * P], ident16[:, :])
                last.then_inc(f_ypose, 1)

            def f_down(m):
                pe.wait_ge(f_yTr, m + 1)
                for j in range(HID0 // P):
                    last = mm(pf1[:, 0:D], f_yqT[:, j, :], c_wout[:, j, :], start=j == 0, stop=j == HID0 // P - 1)
                last.then_inc(f_o, 1)

            def b_transpose(m):
                if first(m):
                    pe.wait_ge(w_b, LOADS_B)
                pe.wait_ge(f_out, m + 1)
                after_previous(pe, b_yread, m)
                xpose_rows(pb0, b_in, b_xpose)

            def b_project(m):
                pe.wait_ge(b_xTr, m + 1)
                for kt in range(KT):
                    last = mm(pb0[:, 0:QKV1], b_xT[:, kt, :], c_wqkv1[:, kt, :], start=kt == 0, stop=kt == KT - 1)
                last.then_inc(b_qkv, 1)

            def b_transpose_qk(m):
                pe.wait_ge(b_rot, m + 1)
                k = k_rep[:, :, :, :].rearrange("p g r d -> p (g r d)")
                xpose_rows(pb0, q_rot[:, :, :].rearrange("p h d -> p (h d)"), b_qpose)
                xpose_rows(pb1, k, b_kpose)

            def b_scores(m):
                pe.wait_ge(b_qTr, m + 1)
                pe.wait_ge(b_kBDr, m + 1)
                for b in range(2):
                    rows = slice(b * TP, (b + 1) * TP)
                    for dst, kt, kbd, n in ((pb0, 0, kBD_lo, 2 * REP), (pb1, 1, kBD_hi, REP)):
                        last = mm(dst[rows, 0:n * T].rearrange("p (h s) -> p h s", h=n), qT1[:, kt, rows],
                                  kbd[:, :, b * TP:b * TP + T])
                last.then_inc(b_s, 1)

            def b_probs_transpose(m):
                pe.wait_ge(b_exp, m + 1)
                for j in range(H1 // 2):
                    last = xpose((pb0, pb1)[j // 4][:, (j % 4) * P:(j % 4 + 1) * P],
                                 p1[:, 2 * j:2 * j + 2, :].rearrange("p h s -> p (h s)"))
                last.then_inc(b_pt, 1)

            def b_values(m):
                pe.wait_ge(b_ptr, m + 1)
                for b in range(2):
                    rows = slice(b * TP, (b + 1) * TP)
                    for j in range(H1 // 2):
                        last = mm(pb0[rows, j * 2 * (HD + 1):(j + 1) * 2 * (HD + 1)], pT1[:, j, rows],
                                  vBD[:, b, j // 2, :, :].rearrange("p a d -> p (a d)"))
                last.then_inc(b_o, 1)

            def b_transpose_o(m):
                pe.wait_ge(b_or, m + 1)
                xpose_rows(pb1, o1[:, :, :].rearrange("p h d -> p (h d)"), b_opose)

            def b_output(m):
                pe.wait_ge(b_oTr, m + 1)
                for kt in range(KT):
                    last = mm(pb0[:, 0:D], oT1[:, kt, :], c_wo1[:, kt, :], start=kt == 0, stop=kt == KT - 1)
                last.then_inc(b_y, 1)

            def r_transpose(m):
                pe.wait_ge(b_out, m + 1)
                ahead = m + R_BEHIND + 1
                pe.wait_ge(a_v2r, min(ahead, TILES) if isinstance(m, int) else ahead)
                xpose_rows(pa0, moe_now, r_xpose)

            def r_route(m):
                pe.wait_ge(r_xTr, m + 1)
                for kt in range(KT):
                    last = mm(pa0[:, LG:LG + NE], r_xT[:, kt, :], c_rw[:, kt, :], start=kt == 0, stop=kt == KT - 1)
                last.then_inc(r_l, 1)

            def r_rank(m):
                pe.wait_ge(r_onehot, m + 1)
                mm(pa0[:, RK:RK + NE + 1], c_tri[:, :], chosen[:, :])
                mm(pa0[:, TT:TT + NE + 1], ones[:, :], chosen[:, :]).then_inc(r_ranked, 1)

            pe.wait_ge(w_t, LOADS_T)
            overlapped(pe, (
                (4, b_transpose), (2, a_transpose), (4, b_project), (2, a_project_q), (1, t_transpose),
                (4, b_transpose_qk), (2, a_project_k), (2, a_relative_lo), (4, b_scores), (2, a_relative_hi),
                (3, f_transpose_x), (2, a_scores), (3, f_up_gate), (1, t_pointwise), (2, a_project_v),
                (4, b_probs_transpose), (2, a_project_v_rest), (4, b_values), (1, t_dft), (3, f_transpose_y),
                (4, b_transpose_o), (1, t_dft_seq), (2, a_probs_transpose), (4, b_output), (5, r_transpose),
                (3, f_down), (2, a_values), (5, r_route), (2, a_output), (5, r_rank)))
            def expert(j):
                at = plan[0:1, j:j + 1] if isinstance(j, int) else plan[0:1, bass.ds(j, 1)]
                return pe.value_load(at, min_val=0, max_val=NE - 1)

            def weights(w, e, kt, rows=P):
                return w[0:rows, bass.ds(e, 1), kt, :].rearrange("p a n -> p (a n)")

            def e_transpose(j):
                pe.wait_ge(e_loaded, 16 * j + 16)
                after_previous(pe, e_xTr, j)
                xpose_rows(pt, e_tok, e_xpose)

            def e_gate_up(j):
                e = expert(j)
                pe.wait_ge(w_ready, e + 1)
                pe.wait_ge(e_xTr, j + 1)
                after_previous(pe, e_yr, j)
                for w, dst, sig in ((w1_sb, pa0, e_g), (w2_sb, pa1, e_u)):
                    mm(dst[:, :], e_xT[:, 0, :], weights(w, e, 0), stop=False)
                    mm(dst[:, :], e_xT[0:KB, 1, :], weights(w, e, 1, KB), start=False).then_inc(sig, 1)

            def e_transpose_y(j):
                pe.wait_ge(e_yr, j + 1)
                for k in range(HID1 // P):
                    last = xpose(pb0[:, k * P:(k + 1) * P], e_y[:, k * P:(k + 1) * P])
                last.then_inc(e_ypose, 1)

            def e_down(j):
                e = expert(j)
                pe.wait_ge(e_yTr, j + 1)
                after_previous(pe, e_or, j)
                for k in range(HID1 // P):
                    last = mm(pb1[:, 0:D], e_yT[:, k, :], weights(w3_sb, e, k), start=k == 0, stop=k == HID1 // P - 1)
                last.then_inc(e_o, 1)

            pe.wait_ge(w_e, 16)
            staggered(pe, (("y", e_transpose_y), ("g", e_gate_up), ("x", e_transpose), ("y", e_down)))

        @block.scalar
        def _(act):
            def copy(dst, src):
                return nc.scalar.activation(dst, src, ACT.Copy)

            def copy_rows(dst, src, sig):
                copy(dst[:, 0, :], src[:, 0:P])
                copy(dst[0:KB, 1, :], src[0:KB, P:2 * P]).then_inc(sig, 1)

            def prepare():
                act.wait_ge(rk_done, 1)
                act.wait_ge(cleared, 3)
                rk = pa0[:, 0:HP * REL].rearrange("p (h r) -> p h r", h=HP)
                copy(rkBD[0:TP, :, 0, :], rk[0:TP])
                copy(rkBD[TP:P, :, 1, :], rk[TP:P]).then_inc(rk_stored, 1)
                act.wait_ge(w_f, LOADS_F)
                w = c_win_f[:, :, :].rearrange("p a b -> p (a b)")
                nc.scalar.activation(c_win[:, :, :].rearrange("p a b -> p (a b)"), w, ACT.Abs, accum_out=wsum[:, 0:1]).then_inc(wabs, 1)
                w = c_wout_f[:, :, :].rearrange("p a b -> p (a b)")
                nc.scalar.activation(c_wout[:, :, :].rearrange("p a b -> p (a b)"), w, ACT.Abs, accum_out=wsum[:, 1:2]).then_inc(wabs, 1)

            def t_copy_x(m):
                if first(m):
                    act.wait_ge(cleared_dve, 3)
                act.wait_ge(t_xpose, m + 1)
                copy(xT_lo[:, :, HALO:HALO + SEQ], pt[:, 0:2 * SEQ].rearrange("p (b s) -> p b s", b=2))
                for b in range(2):
                    last = copy(xT_hi[b * KB:(b + 1) * KB, HALO:HALO + SEQ], pt[0:KB, (2 + b) * SEQ:(3 + b) * SEQ])
                last.then_inc(t_xT, 1)

            def t_middle_tap(m):
                act.wait_ge(t_xpose, m + 1)
                tap, bias = (c_taps[:, :, k:k + 1] for k in (HALO, TAPS))
                nc.scalar.activation(conv_lo[:, :, :], pt[:, 0:2 * SEQ].rearrange("p (b s) -> p b s", b=2)[:, :, 0:PAIRS],
                                     ACT.Identity, scale=tap[:, 0, :], bias=bias[:, 0, :])
                for b in range(2):
                    r = slice(b * KB, (b + 1) * KB)
                    last = nc.scalar.activation(conv_hi[r, :], pt[0:KB, (2 + b) * SEQ:(2 + b) * SEQ + PAIRS],
                                                ACT.Identity, scale=tap[r, 1, :], bias=bias[r, 1, :])
                last.then_inc(t_mtap, 1)

            def t_relu(m):
                act.wait_ge(t_pooled, m + 1)
                nc.scalar.activation(hT[:, 0, :, 0:T], pooled[:, 0, :, :], ACT.Relu, bias=c_bpw[:, 0:1])
                nc.scalar.activation(hT[0:KB, 1, :, 0:T], pooled[0:KB, 1, :, :], ACT.Relu,
                                     bias=c_bpw[0:KB, 1:2]).then_inc(t_h, 1)

            def t_copy_z(m):
                act.wait_ge(t_z, m + 1)
                copy(z_sb[:, :], pt[:, 0:2 * D]).then_inc(t_zs, 1)

            def a_copy_x(m):
                if first(m):
                    prepare()
                act.wait_ge(a_xpose, m + 1)
                copy_rows(a_xT, pa0, a_xTr)

            def a_copy_q(m):
                act.wait_ge(a_q, m + 1)
                nc.scalar.activation(q8[:, :, :].rearrange("p a b -> p (a b)"), pa0[:, :], ACT.Copy,
                                     scale=DK ** -0.5).then_inc(a_q8r, 1)

            def a_q_blocks(m):
                act.wait_ge(a_q8r, m + 1)
                after_previous(act, a_s, m)
                for hp in range(HP):
                    for h2 in range(2):
                        r = slice(h2 * TP, (h2 + 1) * TP)
                        last = nc.scalar.activation(
                            qBD[r, hp, :, h2, :], q8[r, hp, :].rearrange("p (b t) -> p b t", b=2),
                            ACT.Identity, bias=c_bias_q[r, 0, hp:hp + 1])
                last.then_inc(a_qbd, 1)

            def a_copy_k(m):
                act.wait_ge(a_k, m + 1)
                after_previous(act, a_s, m)
                copy(kT0[:, :, :].rearrange("p a b -> p (a b)"), pa0[:, :]).then_inc(a_kr, 1)

            def a_copy_v(m):
                act.wait_ge(a_v1, m + 1)
                after_previous(act, a_o, 2 * m)
                copy(v0[:, 0:512], pa0[:, :]).then_inc(a_v1r, 1)

            def a_copy_v_rest(m):
                act.wait_ge(a_v2, m + 1)
                copy(v0[:, 512:H0 * DV], pa0[:, 0:H0 * DV - 512]).then_inc(a_v2r, 1)

            def a_copy_rel(i, src):
                def stage(m):
                    if i == 0:
                        after_previous(act, a_wr, 16 * m)
                    act.wait_ge(a_r, 2 * m + 1 + i)
                    copy(rel_tok[:, :, :, 2 * i:2 * i + 2].rearrange("p a r h -> p h a r"),
                         src[:, 0:4 * REL].rearrange("p (h a r) -> p h a r", h=2, a=2)).then_inc(a_rs, 1)
                return stage
            a_copy_rel_lo, a_copy_rel_hi = a_copy_rel(0, pa0), a_copy_rel(1, pa0)

            def a_expo(m):
                act.wait_ge(a_shift, m + 1)
                for h in range(H0):
                    last = nc.scalar.activation(p0[:, h // 2, h % 2, 0:T], s0[:, h, :], ACT.Exp, bias=max0[:, h:h + 1],
                                                accum_out=sum0[:, h:h + 1])
                last.then_inc(a_exp, 1)

            def a_copy_probs(m):
                act.wait_ge(a_pt, m + 1)
                for b in range(2):
                    r = slice(b * TP, (b + 1) * TP)
                    last = copy(pT0[r, :, b, :], pa2[r, :].rearrange("p (h t) -> p h t", h=H0))
                last.then_inc(a_ptr, 1)

            def a_copy_heads(i, src):
                def stage(m):
                    act.wait_ge(a_o, 2 * m + 1 + i)
                    copy(oT0[0:DV, 4 * i:4 * i + 4, :].rearrange("p h t -> p (h t)"), src[0:DV, :]).then_inc(a_or, 1)
                return stage
            a_copy_heads_lo, a_copy_heads_hi = a_copy_heads(0, pa1), a_copy_heads(1, pa2)

            def f_square_x(m):
                act.wait_ge(a_out, m + 1)
                nc.scalar.activation(f_sq[:, 0:D], f_in[:, :], ACT.Square, accum_out=ssq["x"][:, :]).then_inc(var_ready["x"], 1)

            def f_copy_x(m):
                act.wait_ge(f_xpose, m + 1)
                d = pf0[:, :].bitcast(BF16)
                copy_rows(f_xqT, d, f_xTr)

            def f_tanh_gate(m):
                act.wait_ge(f_gt, m + 1)
                nc.scalar.activation(f_tanh[:, :], pf1[:, :], ACT.Tanh, scale=dq["x"][:, 1:2]).then_inc(f_tanhr, 1)

            def f_square_y(m):
                act.wait_ge(f_yr, m + 1)
                nc.scalar.activation(f_sq[:, :], f_y[:, :], ACT.Square, accum_out=ssq["y"][:, :]).then_inc(var_ready["y"], 1)

            def f_copy_y(m):
                act.wait_ge(f_ypose, m + 1)
                d = pf0[:, :].bitcast(BF16)
                copy(f_yqT[:, :, :].rearrange("p a b -> p (a b)"), d[:, 0:HID0]).then_inc(f_yTr, 1)

            def b_copy_x(m):
                act.wait_ge(b_xpose, m + 1)
                copy_rows(b_xT, pb0, b_xTr)

            def b_copy_v(m):
                act.wait_ge(b_qkv, m + 1)
                v = pb0[:, (H1 + KV1) * HD:QKV1].rearrange("p (g d) -> p g d", g=KV1)
                for b in range(2):
                    for h2 in range(2):
                        last = copy(vBD[h2 * TP:(h2 + 1) * TP, b, :, h2, 0:HD], v[b * TP:(b + 1) * TP])
                last.then_inc(b_vr, 1)

            def b_copy_q(m):
                act.wait_ge(b_qpose, m + 1)
                nc.scalar.activation(qT1[:, 0, :], pb0[:, 0:P], ACT.Copy, scale=SCALE1)
                nc.scalar.activation(qT1[0:KB, 1, :], pb0[0:KB, P:2 * P], ACT.Copy, scale=SCALE1).then_inc(b_qTr, 1)

            def b_expo(m):
                act.wait_ge(b_shift, m + 1)
                for h in range(H1):
                    src, at = (pb0, h) if h < 2 * REP else (pb1, h - 2 * REP)
                    last = nc.scalar.activation(p1[:, h, 0:T], src[:, at * T:(at + 1) * T], ACT.Exp, bias=max1[:, h:h + 1])
                last.then_inc(b_exp, 1)

            def b_keep(m):
                act.wait_ge(b_yread, m + 1)
                row = resid[:, m, :] if isinstance(m, int) else resid[:, bass.ds(m, 1), :].rearrange("p a d -> p (a d)")
                copy(row, res_m[:, :]).then_inc(b_kept, 1)

            def b_copy_probs(m):
                act.wait_ge(b_pt, m + 1)
                copy(pT1[:, 0:4, :].rearrange("p a b -> p (a b)"), pb0[:, :])
                copy(pT1[:, 4:6, :].rearrange("p a b -> p (a b)"), pb1[:, 0:2 * P]).then_inc(b_ptr, 1)

            def b_copy_o(m):
                act.wait_ge(b_opose, m + 1)
                copy_rows(oT1, pb1, b_oTr)

            def r_copy_x(m):
                act.wait_ge(r_xpose, m + 1)
                copy_rows(r_xT, pa0, r_xTr)

            def r_expo(m):
                act.wait_ge(r_max, m + 1)
                nc.scalar.activation(r_exp[:, :], lg[:, :], ACT.Exp, bias=neg_max[:, :],
                                     accum_out=exp_sum[:, :]).then_inc(r_sum, 1)

            overlapped(act, (
                (4, b_copy_x), (2, a_copy_x), (4, b_copy_v), (2, a_copy_q), (1, t_copy_x), (1, t_middle_tap),
                (3, f_square_x), (2, a_copy_k), (4, b_copy_q), (2, a_q_blocks), (2, a_copy_rel_lo),
                (2, a_copy_rel_hi), (3, f_copy_x), (3, f_tanh_gate), (4, b_expo), (3, f_square_y), (2, a_copy_v),
                (1, t_relu), (4, b_copy_probs), (2, a_expo), (1, t_copy_z), (4, b_copy_o), (2, a_copy_v_rest),
                (3, f_copy_y), (2, a_copy_probs), (2, a_copy_heads_lo), (5, r_copy_x), (2, a_copy_heads_hi),
                (5, r_expo), (4, b_keep)))
            def e_copy_x(j):
                act.wait_ge(e_xpose, j + 1)
                copy_rows(e_xT, pt, e_xTr)

            def e_tanh_gate(j):
                act.wait_ge(e_g, j + 1)
                nc.scalar.activation(e_tanh[:, :], pa0[:, :], ACT.Tanh, scale=0.5).then_inc(e_tanhr, 1)

            def e_copy_y(j):
                act.wait_ge(e_ypose, j + 1)
                copy(e_yT[:, :, :].rearrange("p a b -> p (a b)"), pb0[:, :]).then_inc(e_yTr, 1)

            def e_store(j):
                dst = answered[P * j:P * j + P, :] if isinstance(j, int) else answered[bass.ds(act.snap(P * j), P), :]
                act.wait_ge(e_or, j + 1)
                act.dma_start(dst, e_out[:, :]).then_inc(e_stored, 16)
            staggered(act, (("y", e_copy_y), ("g", e_tanh_gate), ("x", e_copy_x), ("y", e_store)))

        @block.vector
        def _(dve):
            v = nc.vector
            ch = {k: Chain(dve, chains[f"dve_{k}"]) for k in "tafbr"}

            n_setup = [0]

            def setup(ins):
                n_setup[0] += 1
                ins.then_inc(setup_dve, 1)
                dve.wait_ge(setup_dve, n_setup[0])
            for t_ in (xT_lo, xT_hi, hT):
                v.memset(t_[tuple(slice(None) for _ in t_.shape)], 0.0).then_inc(cleared_dve, 1)
            dve.wait_ge(w_t, LOADS_T)

            def ternary_weights():
                setup(v.tensor_copy(ident16[:, :], ident[:, :]))
                dve.wait_ge(cleared, 1)
                for h2 in range(2):
                    setup(v.memset(vBD[h2 * TP:(h2 + 1) * TP, :, :, h2, HD:HD + 1], 1.0))
                dve.wait_ge(wtotal, 1)
                setup(v.tensor_scalar(wsc[:, 0:1], pf0[:, 0:1], 1.0 / (2 * HID0 * D), EPS, ALU.mult, ALU.max))
                setup(v.tensor_scalar(wsc[:, 1:2], pf0[:, 1:2], 1.0 / (HID0 * D), EPS, ALU.mult, ALU.max))
                setup(v.reciprocal(wsc[:, 2:4], wsc[:, 0:2]))
                for i, (w, q) in enumerate(((c_win_f, c_win), (c_wout_f, c_wout))):
                    w, q = (z[:, :, :].rearrange("p a b -> p (a b)") for z in (w, q))
                    setup(v.tensor_scalar(w, w, wsc[:, 2 + i:3 + i], MAGIC, ALU.mult, ALU.add))
                    setup(v.tensor_scalar(w, w, MAGIC + 1, MAGIC - 1, ALU.min, ALU.max))
                    ins = v.tensor_scalar(q, w, MAGIC, None, ALU.subtract)
                    setup(ins) if i == 0 else ins.then_inc(wtern, 1)
                dve.wait_ge(wtern, 1)

            def moments(c, k, src):
                c.link(v.bn_stats(st[k][:, :], src))
                v.memset(spare[:, :], 0.0)
                v.bn_aggr(mv[k][:, :], st[k][:, :]).then_inc(var_ready[k], 1)

            def t_convolve(m, taps_now):
                c = ch["t"]
                if taps_now[0] == 0:
                    dve.wait_ge(t_xT, m + 1)
                    dve.wait_ge(t_mtap, m + 1)
                for k in taps_now:
                    if k == HALO:
                        continue
                    if k:
                        c.wait(back=1)
                    c.mark(v.scalar_tensor_tensor(conv_lo[:, :, :], xT_lo[:, :, k:k + PAIRS], c_taps[:, 0, k:k + 1],
                                                  conv_lo[:, :, :], ALU.mult, ALU.add))
                    if k:
                        c.wait(back=1)
                    ins = v.scalar_tensor_tensor(conv_hi[:, :], xT_hi[:, k:k + PAIRS], c_taps[:, 1, k:k + 1],
                                                 conv_hi[:, :], ALU.mult, ALU.add)
                    if k < TAPS - 1:
                        c.mark(ins)
                    else:
                        ins.then_inc(t_conv, 1)

            def t_convolve_1(m):
                ch["t"].stage("conv1", m)
                t_convolve(m, (0, 1, 2))

            def t_convolve_2(m):
                ch["t"].stage("conv2", m)
                t_convolve(m, (4, 5, 6))

            def t_pool(m):
                dve.wait_ge(t_pw, m + 1)
                v.tensor_reduce(pooled[:, 0, :, :].rearrange("p b s -> p (b s)"),
                                pt[:, 0:2 * PAIRS].rearrange("p (s two) -> p s two", two=2), axis=AX.X, op=ALU.max)
                v.tensor_reduce(pooled[0:KB, 1, :, :].rearrange("p b s -> p (b s)"),
                                pt[0:KB, 2 * PAIRS:4 * PAIRS].rearrange("p (s two) -> p s two", two=2),
                                axis=AX.X, op=ALU.max).then_inc(t_pooled, 1)

            def t_moments(m):
                ch["t"].stage("moments", m)
                dve.wait_ge(t_y, m + 1)
                moments(ch["t"], "t1", pt[:, 0:D])
                dve.wait_ge(var_ready["t1"], m + 1)
                after_previous(dve, a_kept, m)
                v.scalar_tensor_tensor(res_a[:, :], pt[:, 0:D], mv["t1"][:, 0:1], c_gamma[:, :],
                                       ALU.subtract, ALU.mult).then_inc(t_yread, 1)

            def t_norm(m):
                c = ch["t"]
                c.stage("norm", m)
                dve.wait_ge(t_yread, m + 1)
                dve.wait_ge(rstd_ready["t1"], m + 1)
                c.link(v.scalar_tensor_tensor(res_a[:, :], res_a[:, :], rstd["t1"][:, :], c_beta[:, :],
                                              ALU.mult, ALU.add))
                moments(c, "t2", res_a[:, :])

            def a_bias_q(m):
                dve.wait_ge(a_q8r, m + 1)
                after_previous(dve, a_r, 2 * m)
                v.tensor_tensor(qr[:, :, :], q8[:, :, :], c_bias_q[:, 1, :].unsqueeze(2).broadcast_to([P, HP, P]),
                                ALU.add).then_inc(a_qrr, 1)

            def a_max_scores(m):
                c = ch["a"]
                c.stage("max", m)
                dve.wait_ge(a_s, m + 1)
                dve.wait_ge(a_rel, 32 * m + 32)
                c.link(v.tensor_tensor(s0[:, :, :].rearrange("p (h b) s -> p h b s", h=HP),
                                       pa1[:, 0:H0 * T].rearrange("p (h b s) -> p h b s", h=HP, b=2),
                                       rel_skew[:, :, :, :].rearrange("p b s h -> p h b s"), ALU.add))
                v.tensor_reduce(max0[:, :], s0[:, :, :], axis=AX.X, op=ALU.max, negate=True).then_inc(a_shift, 1)

            def a_normalise(m):
                c = ch["a"]
                c.stage("normalise", m)
                probs = p0[:, :, :, 0:T].rearrange("p h b s -> p (h b) s")
                dve.wait_ge(a_exp, m + 1)
                c.link(v.reciprocal(inv0[:, :], sum0[:, :]))
                v.tensor_tensor(probs, probs, inv0[:, :].unsqueeze(2).broadcast_to([P, H0, T]),
                                ALU.mult).then_inc(a_p, 1)

            def a_residual(m):
                c = ch["a"]
                c.stage("residual", m)
                dve.wait_ge(a_y, m + 1)
                dve.wait_ge(a_kept, m + 1)
                v.tensor_tensor(res_f[:, :], hold_a[:, :], pa1[:, 0:D], ALU.add).then_inc(a_yread, 1)
                dve.wait_ge(a_yread, m + 1)
                moments(c, "a", res_f[:, :])

            def quantise(c, m, k, src, gain, work, dst, done):
                dve.wait_ge(rstd_ready[k], m + 1)
                c.link(v.scalar_tensor_tensor(work, src, rstd[k][:, :], gain, ALU.mult, ALU.mult))
                c.link(v.tensor_reduce(amax[k][:, :], work, axis=AX.X, op=ALU.max, apply_absolute_value=True))
                c.link(v.tensor_scalar(unit[k][:, :], amax[k][:, :], EPS, 1.0 / 127.0, ALU.max, ALU.mult))
                c.mark(v.reciprocal(qsc[k][:, 0:1], unit[k][:, :]))
                w = wsc[:, 0:1] if k == "x" else wsc[:, 1:2]
                c.mark(v.tensor_tensor(dq[k][:, 0:1], unit[k][:, :], w, ALU.mult))
                c.wait(back=1)
                c.mark(v.tensor_scalar(work, work, qsc[k][:, 0:1], MAGIC, ALU.mult, ALU.add))
                if k == "x":
                    c.wait(back=1)
                    c.mark(v.tensor_scalar(dq[k][:, 1:2], dq[k][:, 0:1], 0.5, None, ALU.mult))
                    c.wait()
                    c.mark(v.tensor_scalar(dq[k][:, 2:3], dq[k][:, 1:2], dq[k][:, 0:1], None, ALU.mult))
                else:
                    c.wait()
                v.tensor_scalar(dst, work, MAGIC + 127, MAGIC, ALU.min, ALU.subtract).then_inc(done, 1)

            def f_quantise_x(m):
                if first(m):
                    ternary_weights()
                ch["f"].stage("quantise_x", m)
                quantise(ch["f"], m, "x", f_in[:, :], c_gin[:, :], f_x[:, :], f_xq[:, :], f_xqr)

            def f_silu(m):
                c = ch["f"]
                c.stage("silu", m)
                dve.wait_ge(f_up, m + 1)
                dve.wait_ge(f_tanhr, m + 1)
                c.link(v.scalar_tensor_tensor(f_gate[:, :], f_tanh[:, :], 1.0, pf1[:, :], ALU.add, ALU.mult))
                v.scalar_tensor_tensor(f_y[:, :], f_gate[:, :], dq["x"][:, 2:3], pf0[:, :], ALU.mult,
                                       ALU.mult).then_inc(f_yr, 1)

            def f_quantise_y(m):
                ch["f"].stage("quantise_y", m)
                quantise(ch["f"], m, "y", f_y[:, :], c_gout[:, :], f_gate[:, :], f_yq[:, :], f_yqr)

            def f_residual(m):
                c = ch["f"]
                c.stage("residual", m)
                dve.wait_ge(f_o, m + 1)
                v.scalar_tensor_tensor(res_b[:, :], pf1[:, 0:D], dq["y"][:, 0:1], res_f[:, :], ALU.mult,
                                       ALU.add).then_inc(f_yread, 1)
                dve.wait_ge(f_yread, m + 1)
                moments(c, "f", res_b[:, :])

            def b_rotate(m):
                if first(m):
                    dve.wait_ge(w_b, LOADS_B)
                    dve.wait_ge(cleared, 3)
                    v.tensor_copy(chosen[:, NE:NE + 1], c_real[:, 1:2]).then_inc(pads_chosen, 1)
                c = ch["b"]
                c.stage("rotate", m)
                dve.wait_ge(b_vr, m + 1)
                n, hd = H1 + KV1, HD // 2
                qk = pb0[:, 0:n * HD].rearrange("p (h d) -> p h d", h=n)
                c.mark(v.tensor_tensor(rot_c[:, :, :], qk, c_rope[:, 0:1, :].broadcast_to([P, n, HD]), ALU.mult))
                c.mark(v.tensor_tensor(rot_s[:, :, 0:hd], qk[:, :, hd:HD],
                                       c_rope[:, 1:2, 0:hd].broadcast_to([P, n, hd]), ALU.mult))
                c.link(v.tensor_tensor(rot_s[:, :, hd:HD], qk[:, :, 0:hd],
                                       c_rope[:, 1:2, hd:HD].broadcast_to([P, n, hd]), ALU.mult))
                v.tensor_tensor(q_rot[:, :, :], rot_c[:, 0:H1, :], rot_s[:, 0:H1, :], ALU.add)
                v.tensor_tensor(k_rep[:, :, :, :], rot_c[:, H1:n, :].unsqueeze(2).broadcast_to([P, KV1, REP, HD]),
                                rot_s[:, H1:n, :].unsqueeze(2).broadcast_to([P, KV1, REP, HD]), ALU.add).then_inc(b_rot, 1)

            def b_key_blocks(m):
                dve.wait_ge(b_kpose, m + 1)
                v.tensor_tensor(kBD_lo[:, :, :], pb1[:, 0:P].unsqueeze(1).broadcast_to([P, 2 * REP, P]),
                                c_blocks[:, :].unsqueeze(2).broadcast_to([P, 2 * REP, P]), ALU.mult)
                v.tensor_tensor(kBD_hi[0:KB, :, :], pb1[0:KB, P:2 * P].unsqueeze(1).broadcast_to([KB, REP, P]),
                                c_blocks[0:KB, 0:REP].unsqueeze(2).broadcast_to([KB, REP, P]),
                                ALU.mult).then_inc(b_kBDr, 1)

            def b_max_scores(m):
                dve.wait_ge(b_s, m + 1)
                for src, lo, n in ((pb0, 0, 2 * REP), (pb1, 2 * REP, REP)):
                    last = v.tensor_reduce(max1[:, lo:lo + n], src[:, 0:n * T].rearrange("p (h s) -> p h s", h=n),
                                           axis=AX.X, op=ALU.max, negate=True)
                last.then_inc(b_shift, 1)

            def b_normalise(m):
                c = ch["b"]
                c.stage("normalise", m)
                dve.wait_ge(b_o, m + 1)
                heads = pb0[:, 0:H1 * (HD + 1)].rearrange("p (h d) -> p h d", h=H1)
                c.link(v.reciprocal(inv1[:, :].unsqueeze(2), heads[:, :, HD:HD + 1]))
                v.tensor_tensor(o1[:, :, :], heads[:, :, 0:HD],
                                inv1[:, :].unsqueeze(2).broadcast_to([P, H1, HD]), ALU.mult).then_inc(b_or, 1)

            def b_residual(m):
                c = ch["b"]
                c.stage("residual", m)
                dve.wait_ge(b_y, m + 1)
                after_previous(dve, b_kept, m)
                after_previous(dve, b_out, m)
                v.tensor_tensor(res_m[:, :], res_b[:, :], pb0[:, 0:D], ALU.add).then_inc(b_yread, 1)
                dve.wait_ge(b_yread, m + 1)
                moments(c, "b", res_m[:, :])

            def r_choose(m):
                c = ch["r"]
                c.stage("choose", m)
                if first(m):
                    dve.wait_ge(pads_chosen, 1)
                dve.wait_ge(r_l, m + 1)
                c.link(v.tensor_tensor(lg[:, :], pa0[:, LG:LG + NE], c_rb[:, :], ALU.add))
                v.tensor_reduce(neg_max[:, :], lg[:, :], axis=AX.X, op=ALU.max, negate=True).then_inc(r_max, 1)
                dve.wait_ge(r_max, m + 1)
                c.link(v.tensor_scalar(best[:, :], lg[:, :], neg_max[:, :], 0.0, ALU.add, ALU.is_ge))
                c.link(v.tensor_tensor(best[:, :], best[:, :], c_prefer[:, :], ALU.mult))
                c.link(v.tensor_reduce(best_one[:, :], best[:, :], axis=AX.X, op=ALU.max))
                v.tensor_scalar(chosen[:, 0:NE], best[:, :], best_one[:, :], c_real[:, 0:1], ALU.is_equal,
                                ALU.mult).then_inc(r_onehot, 1)

            def r_slots(m):
                c = ch["r"]
                c.stage("slots", m)
                dve.wait_ge(r_ranked, m + 1)
                c.link(v.tensor_tensor(place[:, :], filled[:, :], pa0[:, RK:RK + NE + 1], ALU.add))
                c.link(v.tensor_tensor(filled[:, :], filled[:, :], pa0[:, TT:TT + NE + 1], ALU.add))
                v.scalar_tensor_tensor(place_one[:, :], place[:, :], 1.0, chosen[:, :], ALU.mult, ALU.mult,
                                       accum_out=slot_f[:, :]).then_inc(r_read, 1)
                dve.wait_ge(r_read, m + 1)
                dve.wait_ge(r_sum, m + 1)
                v.tensor_copy(slot_now[:, :], slot_f[:, :]).then_inc(r_slot, 1)
                if isinstance(m, int):
                    v.tensor_copy(slots[:, m:m + 1], slot_f[:, :])
                    v.reciprocal(max_prob[:, m:m + 1], exp_sum[:, :]).then_inc(r_kept, 1)
                else:
                    v.tensor_copy(slots[:, bass.ds(m, 1)], slot_f[:, :])
                    v.reciprocal(max_prob[:, bass.ds(m, 1)], exp_sum[:, :]).then_inc(r_kept, 1)

            overlapped(dve, (
                (4, b_rotate), (2, a_bias_q), (4, b_key_blocks), (1, t_convolve_1), (3, f_quantise_x),
                (1, t_convolve_2), (4, b_max_scores), (3, f_silu), (1, t_pool), (2, a_max_scores), (3, f_quantise_y),
                (4, b_normalise), (2, a_normalise), (1, t_moments), (4, b_residual), (3, f_residual), (1, t_norm),
                (5, r_choose), (5, r_slots), (2, a_residual)))
            n_plan = [n_setup[0]]

            def plan_step(ins):
                n_plan[0] += 1
                ins.then_inc(setup_dve, 1)
                dve.wait_ge(setup_dve, n_plan[0])
            dve.wait_ge(r_scattered, 16 * TILES)
            plan_step(v.tensor_tensor(tiles_of[:, :], filled[:, 0:NE], c_region[:, 0:NE], ALU.subtract))
            plan_step(v.tensor_scalar(tiles_of[:, :], tiles_of[:, :], 1.0 / P, (P - 1) / P - 0.5 + 0.5 / P, ALU.mult, ALU.add))
            plan_step(v.tensor_scalar(tiles_of[:, :], tiles_of[:, :], MAGIC, None, ALU.add))
            plan_step(v.tensor_scalar(tiles_of[:, :], tiles_of[:, :], MAGIC, None, ALU.subtract))
            plan_step(v.memset(tiles_before[:, 0:1], 0.0))
            for e in range(NE):
                plan_step(v.tensor_tensor(tiles_before[:, e + 1:e + 2], tiles_before[:, e:e + 1], tiles_of[:, e:e + 1], ALU.add))
            plan_step(v.tensor_scalar(jump[:, :], tiles_of[:, :], -float(P), float(CAP), ALU.mult, ALU.add))
            plan_step(v.memset(plan_f[:, EXPERT:EXPERT + MAX_TILES], 0.0))
            plan_step(v.tensor_scalar(plan_f[:, FIRST_ROW:FIRST_ROW + MAX_TILES], c_steps[:, :], float(P), None, ALU.mult))
            for e in range(1, NE):
                plan_step(v.tensor_scalar(reached[:, :], c_steps[:, :], tiles_before[:, e:e + 1], None, ALU.is_ge))
                at = plan_f[:, EXPERT:EXPERT + MAX_TILES]
                plan_step(v.tensor_tensor(at, at, reached[:, :], ALU.add))
                at = plan_f[:, FIRST_ROW:FIRST_ROW + MAX_TILES]
                plan_step(v.scalar_tensor_tensor(at, reached[:, :], jump[:, e - 1:e], at, ALU.mult, ALU.add))
            plan_step(v.tensor_copy(plan_f[:, PAD_ROW:PAD_ROW + NE], filled[:, 0:NE]))
            for k in range(3):
                plan_step(v.tensor_scalar(plan_f[:, STEPS + k:STEPS + k + 1], tiles_before[:, NE:NE + 1], float(k), None, ALU.subtract))
            plan_step(v.memset(e_xT[:, 1, :], 0.0))
            v.tensor_copy(plan[:, :], plan_f[:, :]).then_inc(planned, 1)
            e_chain = Chain(dve, chains["dve_m"])

            def e_silu(j):
                c = e_chain
                c.stage("silu", j)
                dve.wait_ge(e_tanhr, j + 1)
                c.link(v.scalar_tensor_tensor(e_gate[:, :], e_tanh[:, :], 1.0, pa0[:, :], ALU.add, ALU.mult))
                dve.wait_ge(e_u, j + 1)
                after_previous(dve, e_ypose, j)
                v.scalar_tensor_tensor(e_y[:, :], e_gate[:, :], 0.5, pa1[:, :], ALU.mult, ALU.mult).then_inc(e_yr, 1)

            def e_round(j):
                dve.wait_ge(e_o, j + 1)
                after_previous(dve, e_stored, 16 * j)
                v.tensor_copy(e_out[:, :], pb1[:, 0:D]).then_inc(e_or, 1)
            for e in range(1, NE + 1):
                plan_step(v.tensor_scalar(slot_past[:, :], slots[:, :], float(e * CAP), jump[:, e - 1:e], ALU.is_ge, ALU.mult))
                plan_step(v.tensor_tensor(answer_at_f[:, :], slots[:, :] if e == 1 else answer_at_f[:, :], slot_past[:, :],
                                          ALU.subtract))
            v.tensor_copy(answer_at[:, :], answer_at_f[:, :]).then_inc(located, 1)
            total_steps = staggered(dve, (("g", e_silu), ("y", e_round)))
            dve.wait_ge(e_stored, 16 * total_steps)
            v.memset(e_spare[:, :], 0.0).then_inc(all_stored, 1)
            for g in range(GROUPS):
                ts = slice(g * GT, (g + 1) * GT)
                said = weighted[:, :, :]
                if g:
                    dve.wait_ge(finished, g)
                dve.wait_ge(gathered[g], 16 * GT)
                v.tensor_tensor(said, experts_said[:, ts, :], max_prob[:, ts].unsqueeze(2).broadcast_to([P, GT, D]),
                                ALU.mult).then_inc(scaled, 1)
                dve.wait_ge(scaled, g + 1)
                v.tensor_tensor(resid[:, ts, :], resid[:, ts, :], said, ALU.add).then_inc(finished, 1)


def _tables():
    import numpy as np
    c = {}
    ang = 2 * np.pi * np.outer(np.arange(D), np.arange(D)) / D
    full = np.concatenate([np.cos(ang), np.sin(ang)], 1)
    dft = np.zeros((P, KT, 2 * D), np.float32)
    dft[:, 0], dft[:KB, 1] = full[:P], full[P:]
    c["dft"] = dft
    ang = 2 * np.pi * np.outer(np.arange(T), np.arange(T)) / T
    seq = np.zeros((P, 2, P), np.float32)
    for b in range(2):
        s = slice(b * TP, b * TP + T)
        seq[s, 0, s], seq[s, 1, s] = np.cos(ang), -np.sin(ang)
    c["dft_seq"] = seq
    nb = NF // 2
    width = np.exp(np.log(T + 1) / nb).astype(np.float32) ** np.arange(1, nb + 1, dtype=np.float32) - np.float32(1)
    pos = np.arange(-T + 1, T, dtype=np.float32)
    near = (width[None, :] > np.abs(pos)[:, None]).astype(np.float32)
    c["rk_feat"] = np.ascontiguousarray(np.concatenate([near, np.sign(pos)[:, None] * near], 1).T)
    inv_freq = (1.0 / 10000.0 ** (np.arange(0, HD, 2, dtype=np.float32) / HD)).astype(np.float32)
    f = np.outer(np.arange(T, dtype=np.float32), inv_freq).astype(np.float32)
    rope = np.zeros((P, 2, HD), np.float32)
    for b in range(2):
        s = slice(b * TP, b * TP + T)
        rope[s, 0], rope[s, 1] = np.tile(np.cos(f), (1, 2)), np.concatenate([-np.sin(f), np.sin(f)], 1)
    c["rope"] = rope
    c["blocks"] = (np.arange(P)[:, None] // HD == np.arange(2 * REP)[None, :]).astype(np.float32)
    c["ident"] = np.eye(P, dtype=np.float32)
    c["tri"] = np.triu(np.ones((P, P), np.float32), 1)
    lanes = np.arange(P) % TP < T
    real = np.zeros((P, 2), np.float32)
    real[:, 0], real[:, 1] = lanes, ~lanes
    c["real"] = real
    c["prefer"] = np.ascontiguousarray(np.broadcast_to(np.arange(NE, 0, -1, dtype=np.float32), (P, NE)))
    c["region"] = np.ascontiguousarray(np.broadcast_to(np.arange(NE + 1, dtype=np.float32) * CAP, (P, NE + 1)))
    c["steps"] = np.ascontiguousarray(np.broadcast_to(np.arange(MAX_TILES, dtype=np.float32), (P, MAX_TILES)))
    return c


def _rows(w):
    import numpy as np
    out = np.zeros((P, KT) + w.shape[1:], np.float32)
    out[:, 0], out[:KB, 1] = w[:P], w[P:]
    return out


def kernel(**inputs):
    import numpy as np
    import concourse.bacc as bacc
    from concourse import mybir as mb
    from concourse.bass_utils import run_bass_kernel_spmd as run

    i = {k: np.asarray(v) for k, v in inputs.items()}
    c = _tables()
    wb = np.concatenate([i["L0_tok_w_dw"][:, 0, :], i["L0_tok_b_dw"][:, None]], 1)
    taps = np.stack([wb[:P], np.concatenate([wb[P:], wb[P:]])], 1)
    b_pw = np.zeros((P, KT), np.float32)
    b_pw[:, 0], b_pw[:KB, 1] = i["L0_tok_b_pw"][:P], i["L0_tok_b_pw"][P:]
    wp = i["L0_tok_w_pw"][:, :, 0].T
    w_pw = np.zeros((P, 3, D), np.float32)
    w_pw[:, 0], w_pw[:KB, 1], w_pw[KB:, 2] = wp[:P], wp[P:], wp[P:]
    wo0 = np.zeros((DV + 1, H0, D), np.float32)
    wo0[:DV] = i["L0_attn_Wo"].reshape(H0, DV, D).transpose(1, 0, 2)
    wo0[DV, 0] = i["L0_attn_bo"]
    bias_q = np.stack([i["L0_attn_r_w_bias"].reshape(HP, P).T, i["L0_attn_r_r_bias"].reshape(HP, P).T], 1)
    given = [
        ("x", i["x"]), ("taps", taps), ("w_pw", w_pw), ("b_pw", b_pw), ("dft", c["dft"]), ("dft_seq", c["dft_seq"]),
        ("gamma", i["L0_tok_gamma"]), ("beta", i["L0_tok_beta"]),
        ("wq0", _rows(i["L0_attn_Wq"])), ("wk0", _rows(i["L0_attn_Wk"])), ("wv0", _rows(i["L0_attn_Wv"])),
        ("wo0", wo0), ("rk_feat", c["rk_feat"]), ("wrk", i["L0_attn_Wrk"]), ("bias_q", bias_q),
        ("w_in", _rows(i["L0_ffn_w_in"].T)), ("g_in", i["L0_ffn_g_in"]),
        ("w_out", i["L0_ffn_w_out"].T.reshape(HID0 // P, P, D).transpose(1, 0, 2)), ("g_out", i["L0_ffn_g_out"]),
        ("wqkv1", _rows(np.concatenate([i["L1_attn_Wq"], i["L1_attn_Wk"], i["L1_attn_Wv"]]).T)),
        ("wo1", _rows(i["L1_attn_Wo"].T)), ("rope", c["rope"]), ("blocks", c["blocks"]), ("ident_in", c["ident"]),
        ("router_w", _rows(i["L1_ffn_router_w"])), ("router_b", i["L1_ffn_router_b"]),
        ("w1", i["L1_ffn_w1"]), ("w2", i["L1_ffn_w2"]), ("w3", i["L1_ffn_w3"]),
        ("tri", c["tri"]), ("real", c["real"]), ("prefer", c["prefer"]), ("region", c["region"]), ("steps", c["steps"]),
    ]
    nc = bacc.Bacc("TRN2", target_bir_lowering=False, num_devices=1)
    arrays, args = {}, {}
    for name, a in given:
        a = np.ascontiguousarray(a)
        arrays[f"in_{name}"] = a
        args[name] = nc.dram_tensor(f"in_{name}", a.shape, mb.dt.from_np(a.dtype), kind="ExternalInput").ap()
    args["out"] = nc.dram_tensor("out_0", (NB, T, D), mb.dt.float32, kind="ExternalOutput").ap()
    audio_tower(nc, **args)
    r = run(nc, [arrays], core_ids=[0])
    return r.results[0]["out_0"]
```
